# Optimizing a Trainium2 kernel written in Bass

```python
import numpy as np
import jax
import jax.numpy as jnp

def _softmax(x, axis=-1):
    return jax.nn.softmax(x, axis=axis)

def _gelu(x):
    return jax.nn.gelu(x, approximate=True)

def _silu(x):
    return jax.nn.silu(x)

def _sigmoid(x):
    return jax.nn.sigmoid(x)

def _layernorm(x, axis=-1, eps=1e-05):
    m = jnp.mean(x, axis=axis, keepdims=True)
    v = jnp.var(x, axis=axis, keepdims=True)
    return (x - m) / jnp.sqrt(v + eps)

def _scatter_add(tgt, idx, src, axis=0):
    return tgt.at[idx].add(src)

def _segment_sum(src, seg, n):
    return jax.ops.segment_sum(src, seg, n)
kernel_name = 'mk_macaron_d1_jaxref_r4_f2dfef'

def setup_inputs(seed: int=0):
    np.random.seed(seed)
    _w = jnp.asarray

    def _L0_attn_setup():
        import jax, jax.numpy as jnp
        import numpy as np
        B, N, DIM = (4, 256, 256)
        H, DH = (16, 64)
        NUM_MEM = 4
        TOPK = 64
        QK_SCALE = 10.0

        def l2norm(t, eps=1e-12):
            return t / jnp.clip(jnp.linalg.norm(t, axis=-1, keepdims=True), eps)
        key = jax.random.key(seed)
        ks = jax.random.split(key, 12)
        s = 0.02
        inp = {'x': jax.random.normal(ks[0], (B, N, DIM), dtype=jnp.float32), 'Wq': jax.random.normal(ks[1], (DIM, H * DH), dtype=jnp.float32) * s, 'Wk': jax.random.normal(ks[2], (DIM, H * DH), dtype=jnp.float32) * s, 'Wv': jax.random.normal(ks[3], (DIM, H * DH), dtype=jnp.float32) * s, 'W_pre_th': jax.random.normal(ks[4], (H, H), dtype=jnp.float32) * (1.0 / H) ** 0.5, 'W_post_th': jax.random.normal(ks[5], (H, H), dtype=jnp.float32) * (1.0 / H) ** 0.5, 'mem_k': jax.random.normal(ks[6], (H, NUM_MEM, DH), dtype=jnp.float32), 'mem_v': jax.random.normal(ks[7], (H, NUM_MEM, DH), dtype=jnp.float32), 'head_scale_params': jnp.ones((1, H, 1, 1), dtype=jnp.float32), 'Wg': jax.random.normal(ks[8], (DIM, H * DH), dtype=jnp.float32) * s, 'bg': jnp.ones((H * DH,), dtype=jnp.float32), 'Wo': jax.random.normal(ks[9], (H * DH, DIM), dtype=jnp.float32) * s}
        return inp
    _L0_attn_in = _L0_attn_setup()

    def _L0_ffn_setup():
        import jax, jax.numpy as jnp
        import numpy as np
        B, S, DIM = (4, 1024, 256)
        BASE_COUPLING = 0.1
        NUM_CYCLES = 3

        def _gelu(x):
            return jax.nn.gelu(x, approximate=False)

        def _coupling_net(h, w1, b1, w2, b2, w3, b3, w4, b4):
            h = _gelu(h @ w1 + b1)
            h = _gelu(h @ w2 + b2)
            h = _gelu(h @ w3 + b3)
            return jax.nn.sigmoid(h @ w4 + b4)

        def _global_net(h, w1, b1, w2, b2, w3, b3):
            h = _gelu(h @ w1 + b1)
            h = _gelu(h @ w2 + b2)
            return jax.nn.sigmoid(h @ w3 + b3)

        def _twist(x):
            o_r, o_i, p_r, p_i = jnp.split(x, 4, axis=-1)
            return jnp.concatenate([p_r, -p_i, -o_r, o_i], axis=-1)
        key = jax.random.key(seed)
        ks = jax.random.split(key, 9)
        d = DIM

        def w(k, fan_in, fan_out):
            return jax.random.normal(k, (fan_in, fan_out), dtype=jnp.float32) / np.sqrt(fan_in).astype(np.float32)
        inp = {'x': jax.random.normal(ks[0], (B, S, d), dtype=jnp.float32)}
        cn_dims = [(d, d), (d, d // 2), (d // 2, d // 4), (d // 4, 1)]
        for i, (a, b) in enumerate(cn_dims):
            inp[f'cn_w{i + 1}'] = w(ks[1 + i], a, b)
            inp[f'cn_b{i + 1}'] = jnp.zeros((b,), dtype=jnp.float32)
        gc_dims = [(d, d // 2), (d // 2, d // 4), (d // 4, 1)]
        for i, (a, b) in enumerate(gc_dims):
            inp[f'gc_w{i + 1}'] = w(ks[5 + i], a, b)
            inp[f'gc_b{i + 1}'] = jnp.zeros((b,), dtype=jnp.float32)
        inp['adaptive_range'] = jnp.full((1,), 0.2, dtype=jnp.float32)
        return inp
    _L0_ffn_in = _L0_ffn_setup()
    _d = {'L0_attn_x': _L0_attn_in['x'], 'L0_attn_Wq': _L0_attn_in['Wq'], 'L0_attn_Wk': _L0_attn_in['Wk'], 'L0_attn_Wv': _L0_attn_in['Wv'], 'L0_attn_W_pre_th': _L0_attn_in['W_pre_th'], 'L0_attn_W_post_th': _L0_attn_in['W_post_th'], 'L0_attn_mem_k': _L0_attn_in['mem_k'], 'L0_attn_mem_v': _L0_attn_in['mem_v'], 'L0_attn_head_scale_params': _L0_attn_in['head_scale_params'], 'L0_attn_Wg': _L0_attn_in['Wg'], 'L0_attn_bg': _L0_attn_in['bg'], 'L0_attn_Wo': _L0_attn_in['Wo'], 'L0_ffn_cn_w1': _L0_ffn_in['cn_w1'], 'L0_ffn_cn_b1': _L0_ffn_in['cn_b1'], 'L0_ffn_cn_w2': _L0_ffn_in['cn_w2'], 'L0_ffn_cn_b2': _L0_ffn_in['cn_b2'], 'L0_ffn_cn_w3': _L0_ffn_in['cn_w3'], 'L0_ffn_cn_b3': _L0_ffn_in['cn_b3'], 'L0_ffn_cn_w4': _L0_ffn_in['cn_w4'], 'L0_ffn_cn_b4': _L0_ffn_in['cn_b4'], 'L0_ffn_gc_w1': _L0_ffn_in['gc_w1'], 'L0_ffn_gc_b1': _L0_ffn_in['gc_b1'], 'L0_ffn_gc_w2': _L0_ffn_in['gc_w2'], 'L0_ffn_gc_b2': _L0_ffn_in['gc_b2'], 'L0_ffn_gc_w3': _L0_ffn_in['gc_w3'], 'L0_ffn_gc_b3': _L0_ffn_in['gc_b3'], 'L0_ffn_adaptive_range': _L0_ffn_in['adaptive_range']}
    _x0 = _d['L0_attn_x']
    _d['L0_attn_x'] = jax.random.normal(jax.random.fold_in(jax.random.key(seed), 1), (8, 512, 256), dtype=_x0.dtype)
    del _x0
    return _d

def reference(L0_attn_x, L0_attn_Wq, L0_attn_Wk, L0_attn_Wv, L0_attn_W_pre_th, L0_attn_W_post_th, L0_attn_mem_k, L0_attn_mem_v, L0_attn_head_scale_params, L0_attn_Wg, L0_attn_bg, L0_attn_Wo, L0_ffn_cn_w1, L0_ffn_cn_b1, L0_ffn_cn_w2, L0_ffn_cn_b2, L0_ffn_cn_w3, L0_ffn_cn_b3, L0_ffn_cn_w4, L0_ffn_cn_b4, L0_ffn_gc_w1, L0_ffn_gc_b1, L0_ffn_gc_w2, L0_ffn_gc_b2, L0_ffn_gc_w3, L0_ffn_gc_b3, L0_ffn_adaptive_range):

    def _L0_attn_ref(x, Wq, Wk, Wv, W_pre_th, W_post_th, mem_k, mem_v, head_scale_params, Wg, bg, Wo):
        import jax, jax.numpy as jnp
        import numpy as np
        B, N, DIM = (4, 256, 256)
        H, DH = (16, 64)
        NUM_MEM = 4
        TOPK = 64
        QK_SCALE = 10.0

        def l2norm(t, eps=1e-12):
            return t / jnp.clip(jnp.linalg.norm(t, axis=-1, keepdims=True), eps)
        b, n, _ = x.shape
        q = (x @ Wq).reshape(b, n, H, DH).transpose(0, 2, 1, 3)
        k = (x @ Wk).reshape(b, n, H, DH).transpose(0, 2, 1, 3)
        v = (x @ Wv).reshape(b, n, H, DH).transpose(0, 2, 1, 3)
        mk = jnp.broadcast_to(mem_k[None], (b, H, NUM_MEM, DH))
        mv = jnp.broadcast_to(mem_v[None], (b, H, NUM_MEM, DH))
        k = jnp.concatenate([mk, k], axis=2)
        v = jnp.concatenate([mv, v], axis=2)
        q = l2norm(q)
        k = l2norm(k)
        dots = jnp.einsum('bhid,bhjd->bhij', q, k) * QK_SCALE
        dots = jnp.einsum('hg,bgij->bhij', W_pre_th, dots)
        mask_value = -jnp.finfo(dots.dtype).max
        j = n + NUM_MEM
        col_pos = jnp.arange(j) - NUM_MEM
        causal = jnp.arange(n)[:, None] < col_pos[None, :]
        dots = jnp.where(causal[None, None], mask_value, dots)
        top = jax.lax.top_k(dots, TOPK)[0]
        vk = top[..., -1:]
        dots = jnp.where(dots < vk, mask_value, dots)
        attn = jax.nn.softmax(dots, axis=-1)
        attn = jnp.einsum('hg,bgij->bhij', W_post_th, attn)
        out = jnp.einsum('bhij,bhjd->bhid', attn, v)
        out = out * head_scale_params
        out = out.transpose(0, 2, 1, 3).reshape(b, n, H * DH)
        gates = x @ Wg + bg
        out = out * jax.nn.sigmoid(gates)
        return out @ Wo

    def _L0_ffn_ref(x, cn_w1, cn_b1, cn_w2, cn_b2, cn_w3, cn_b3, cn_w4, cn_b4, gc_w1, gc_b1, gc_w2, gc_b2, gc_w3, gc_b3, adaptive_range):
        import jax, jax.numpy as jnp
        import numpy as np
        B, S, DIM = (4, 1024, 256)
        BASE_COUPLING = 0.1
        NUM_CYCLES = 3

        def _gelu(x):
            return jax.nn.gelu(x, approximate=False)

        def _coupling_net(h, w1, b1, w2, b2, w3, b3, w4, b4):
            h = _gelu(h @ w1 + b1)
            h = _gelu(h @ w2 + b2)
            h = _gelu(h @ w3 + b3)
            return jax.nn.sigmoid(h @ w4 + b4)

        def _global_net(h, w1, b1, w2, b2, w3, b3):
            h = _gelu(h @ w1 + b1)
            h = _gelu(h @ w2 + b2)
            return jax.nn.sigmoid(h @ w3 + b3)

        def _twist(x):
            o_r, o_i, p_r, p_i = jnp.split(x, 4, axis=-1)
            return jnp.concatenate([p_r, -p_i, -o_r, o_i], axis=-1)
        global_context = x.mean(axis=1, keepdims=True)
        gf = _global_net(global_context, gc_w1, gc_b1, gc_w2, gc_b2, gc_w3, gc_b3)
        out = x
        for _ in range(NUM_CYCLES):
            tf = _coupling_net(out, cn_w1, cn_b1, cn_w2, cn_b2, cn_w3, cn_b3, cn_w4, cn_b4)
            combined = 0.7 * gf + 0.3 * tf
            coupling = BASE_COUPLING + adaptive_range * (combined - 0.5) * 2.0
            out = out + coupling * _twist(out)
        return out
    x = L0_attn_x
    x = x + 0.5 * _L0_ffn_ref(_layernorm(x, axis=-1), L0_ffn_cn_w1, L0_ffn_cn_b1, L0_ffn_cn_w2, L0_ffn_cn_b2, L0_ffn_cn_w3, L0_ffn_cn_b3, L0_ffn_cn_w4, L0_ffn_cn_b4, L0_ffn_gc_w1, L0_ffn_gc_b1, L0_ffn_gc_w2, L0_ffn_gc_b2, L0_ffn_gc_w3, L0_ffn_gc_b3, L0_ffn_adaptive_range)
    x = x + _L0_attn_ref(_layernorm(x, axis=-1), L0_attn_Wq, L0_attn_Wk, L0_attn_Wv, L0_attn_W_pre_th, L0_attn_W_post_th, L0_attn_mem_k, L0_attn_mem_v, L0_attn_head_scale_params, L0_attn_Wg, L0_attn_bg, L0_attn_Wo)
    x = x + 0.5 * _L0_ffn_ref(_layernorm(x, axis=-1), L0_ffn_cn_w1, L0_ffn_cn_b1, L0_ffn_cn_w2, L0_ffn_cn_b2, L0_ffn_cn_w3, L0_ffn_cn_b3, L0_ffn_cn_w4, L0_ffn_cn_b4, L0_ffn_gc_w1, L0_ffn_gc_b1, L0_ffn_gc_w2, L0_ffn_gc_b2, L0_ffn_gc_w3, L0_ffn_gc_b3, L0_ffn_adaptive_range)
    return x

_drawn_inputs = setup_inputs


def setup_inputs(seed=0):
    import zlib

    import numpy as np

    out = dict(_drawn_inputs(seed))
    spreads = {'L0_attn_head_scale_params': (1.0, 0.6),
     'L0_attn_bg': (1.0, 0.6),
     'L0_ffn_cn_b1': (0.0, 2.0),
     'L0_ffn_cn_b2': (0.0, 2.0),
     'L0_ffn_cn_b3': (0.0, 2.0),
     'L0_ffn_gc_b1': (0.0, 0.8),
     'L0_ffn_gc_b2': (0.0, 0.8)}
    factors = {'L0_attn_mem_k': 3.057,
     'L0_attn_Wg': 8.0,
     'L0_ffn_cn_w1': 6.332,
     'L0_ffn_cn_w2': 6.633,
     'L0_ffn_cn_w3': 5.318,
     'L0_ffn_cn_w4': 5.936,
     'L0_ffn_gc_w1': 8.0,
     'L0_ffn_gc_w2': 8.0,
     'L0_ffn_gc_w3': 4.821}
    for name, (base, spread) in spreads.items():
        noise = np.random.default_rng([zlib.crc32(name.encode()), seed]).standard_normal(out[name].shape)
        drawn = base * np.exp(spread * noise) if base else spread * noise
        out[name] = jnp.asarray(drawn.astype(out[name].dtype))
    for name, factor in factors.items():
        out[name] = (out[name] * factor).astype(out[name].dtype)
    return out
```

```python
import concourse.bass as bass
from concourse import mybir
from contextlib import ExitStack

F32 = mybir.dt.float32
ALU = mybir.AluOpType
ACT = mybir.ActivationFunctionType
AX = mybir.AxisListType

B, N, D = 8, 512, 256
H, DH, MEM, TOPK = 16, 64, 4, 64
CYCLES = 3
P = 128
TPB = N // P
TILES = B * TPB
IG = 8
GPT = P // IG
GPB = N // IG
PAIRS = H // 2
HD = H * DH
J = N + MEM
LAG = 4
FMAX = float(3.4028234663852886e38)
LN_EPS = 1e-5
QK_SCALE = 10.0


def tiles_of(dram, b):
    return dram[b * N:(b + 1) * N, :].rearrange("(t p) d -> p t d", p=P)


def ffn_phase(nc, tag, X, W, x_dram, out_dram):
    with ExitStack() as c:
        def sb(name, shape):
            return c.enter_context(nc.sbuf_tensor(f"{tag}_{name}", shape, F32))

        def sem(name):
            return c.enter_context(nc.semaphore(f"{tag}_{name}"))

        xn = [sb(f"xn{i}", [P, TPB, D]) for i in range(2)]
        stats = sb("stats", [P, 2, TPB, 6])
        mv = sb("mv", [P, 2, TPB, 2])
        rstd = sb("rstd", [P, 2, TPB])
        ST = sb("state", [P, 2, B, N])
        xsum = sb("xsum", [P, 2, B])
        g1 = sb("g1", [P, B])
        g2 = sb("g2", [64, B])
        gth = sb("gth", [P, B])
        offs = sb("offs", [P, B])
        h1 = [sb(f"h1_{i}", [P, 2, N]) for i in range(2)]
        h2 = [sb(f"h2_{i}", [P, N]) for i in range(2)]
        h3 = [sb(f"h3_{i}", [64, N]) for i in range(2)]
        tf = [sb(f"tf{i}", [P, N]) for i in range(2)]
        cs = sb("cs", [P, N])
        mo = sb("mo", [P, N])
        mp = sb("mp", [P, N])
        bank = [c.enter_context(nc.psum_tensor(f"{tag}_bank{i}", [P, 512], F32)) for i in range(8)]

        x_loaded = sem("x_loaded")
        stats_ready = sem("stats_ready")
        rstd_ready = sem("rstd_ready")
        xn_ready = sem("xn_ready")
        xn_turned = sem("xn_turned")
        state_in = sem("state_in")
        g_mm = sem("g_mm")
        g_act = sem("g_act")
        offs_ready = sem("offs_ready")
        w1_done, w2_done, w3_done, w4_done = (sem(f"w{i}_done") for i in (1, 2, 3, 4))
        h1_ready, h2_ready, h3_ready, tf_ready = (sem(n) for n in ("h1_ready", "h2_ready", "h3_ready", "tf_ready"))
        waited = sem("waited")
        vec = sem("vec")
        upd_done = sem("upd_done")
        back_turned = sem("back_turned")
        x_added = sem("x_added")
        stored = sem("stored")

        block = c.enter_context(nc.Block())
        SKEW = 3

        @block.sync
        def _(sp):
            if x_dram is not None:
                for b in range(B):
                    sp.dma_start(X[:, b * TPB:(b + 1) * TPB, :], tiles_of(x_dram, b)).then_inc(x_loaded, 16)
            for b in range(B):
                sp.wait_ge(x_added, 2 * (b + 1))
                sp.dma_start(tiles_of(out_dram, b), X[:, b * TPB:(b + 1) * TPB, :]).then_inc(stored, 16)
            sp.wait_ge(stored, 16 * B)

        @block.vector
        def _(dve):
            dve.sem_inc(upd_done, B)
            if x_dram is not None:
                dve.wait_ge(x_loaded, 16 * B)
            with dve.Fori(0, B // 2) as r:
                for s in range(2):
                    for t in range(TPB):
                        nc.vector.bn_stats(out=stats[:, s, t, :],
                                           in_=X[:, bass.ds(r * (2 * TPB) + (s * TPB + t), 1), :]).then_inc(vec, 1)
                    dve.wait_ge(vec, r * 16 + 8 * s + 4)
                    dve.sem_inc(waited, 1)
                    for t in range(TPB):
                        last = nc.vector.bn_aggr(out=mv[:, s, t, :], in_=stats[:, s, t, :])
                        last.then_inc(vec, 1)
                    dve.wait_ge(vec, r * 16 + 8 * s + 8)
                    nc.vector.tensor_scalar(mv[:, s, :, 1], mv[:, s, :, 1], LN_EPS, None,
                                            ALU.add).then_inc(stats_ready, 1)
                    dve.wait_ge(rstd_ready, r * 2 + s + 1)
                    dve.wait_ge(xn_turned, r * 2 + s + 1)
                    for t in range(TPB):
                        last = nc.vector.tensor_scalar(
                            xn[s][:, t, :], X[:, bass.ds(r * (2 * TPB) + (s * TPB + t), 1), :],
                            mv[:, s, t, 0:1], rstd[:, s, t:t + 1], ALU.subtract, ALU.mult)
                    last.then_inc(xn_ready, 1)
                    dve.wait_ge(xn_ready, r * 2 + s + 1)
            dve.wait_ge(g_act, 3)
            nc.vector.tensor_scalar(offs[:, :], gth[:, :], W.sgn_ar07[:, 0:1], W.sgn01[:, 0:1], ALU.mult,
                                    ALU.add).then_inc(offs_ready, 1)
            dve.wait_ge(offs_ready, 1)
            with dve.Fori(0, CYCLES) as cyc:
                for b in range(B):
                    at = cyc * (4 * B) + (8 * B + 4 * b)
                    o, p = ST[:, 0, b, :], ST[:, 1, b, :]
                    dve.wait_ge(tf_ready, cyc * B + (b + 2))
                    dve.wait_ge(vec, at)
                    dve.wait_ge(upd_done, cyc * B + (B + b))
                    nc.vector.tensor_scalar(cs[:, :], tf[b % 2][:, :], W.sgn_ar03[:, 0:1], offs[:, b:b + 1],
                                            ALU.mult, ALU.add).then_inc(vec, 1)
                    dve.wait_ge(vec, at + 1)
                    nc.vector.tensor_tensor(mo[:, :], cs[:, :], p, ALU.mult).then_inc(vec, 1)
                    nc.vector.tensor_tensor(mp[:, :], cs[:, :], o, ALU.mult).then_inc(vec, 1)
                    dve.wait_ge(vec, at + 3)
                    nc.vector.tensor_tensor(o, o, mo[:, :], ALU.add).then_inc(vec, 1)
                    nc.vector.tensor_tensor(p, p, mp[:, :], ALU.subtract).then_inc(upd_done, 1)
            for b in range(B):
                for k in range(2):
                    u = 2 * b + k
                    dve.wait_ge(back_turned, u + 1)
                    xt = X[:, b * TPB + 2 * k:b * TPB + 2 * k + 2, :]
                    nc.vector.scalar_tensor_tensor(out=xt, in0=bank[u % 4].rearrange("p (t d) -> p t d", t=2),
                                                   scalar=0.5, in1=xt, op0=ALU.mult,
                                                   op1=ALU.add).then_inc(x_added, 1)

        @block.gpsimd
        def _(pool):
            with pool.Fori(0, B // 2) as r:
                for s in range(2):
                    pool.wait_ge(stats_ready, r * 2 + s + 1)
                    nc.gpsimd.tensor_tensor(rstd[:, s, :], mv[:, s, :, 1], W.neghalf[:, 0:TPB],
                                            ALU.pow).then_inc(rstd_ready, 1)

        @block.tensor
        def _(pe):
            pe.sem_inc(xn_turned, 2)
            with pe.Fori(0, B // 2) as r:
                for s in range(2):
                    pe.wait_ge(xn_ready, r * 2 + s + 1)
                    pe.wait_ge(state_in, r * 4 + (2 * s + 2))
                    for half in range(2):
                        for t in range(TPB):
                            last = nc.tensor.transpose(bank[2 * s + half][:, t * P:(t + 1) * P],
                                                       xn[s][:, t, half * P:(half + 1) * P], W.ident[:, :])
                    last.then_inc(xn_turned, 1)
            pe.wait_ge(state_in, 4 + 2 * B)
            for k in range(2):
                last = nc.tensor.matmul(bank[4][:, 0:B], W.gc_w1[:, k, :], xsum[:, k, :], start=k == 0, stop=k == 1)
            last.then_inc(g_mm, 1)
            pe.wait_ge(g_act, 1)
            nc.tensor.matmul(bank[5][0:64, 0:B], W.gc_w2[:, :], g1[:, :], start=True, stop=True).then_inc(g_mm, 1)
            pe.wait_ge(g_act, 2)
            nc.tensor.matmul(bank[6][:, 0:B], W.gc_w3r[:, :], g2[:, :], start=True, stop=True).then_inc(g_mm, 1)
            pe.wait_ge(g_act, 3)

            with pe.Fori(0, CYCLES) as cyc:
                for k in range(B + SKEW):
                    if k < B:
                        b = k
                        if b >= 2:
                            pe.wait_ge(h1_ready, cyc * (2 * B) + 2 * (b - 1))
                        pe.wait_ge(upd_done, cyc * B + (b + 1))
                        for m in range(2):
                            for kk in range(2):
                                last = nc.tensor.matmul(bank[2 * (b % 2) + m][:, :],
                                                        W.cn_w1[:, kk, m * P:(m + 1) * P], ST[:, kk, b, :],
                                                        start=kk == 0, stop=kk == 1)
                            last.then_inc(w1_done, 1)
                    if 0 <= k - 1 < B:
                        b = k - 1
                        pe.wait_ge(h1_ready, cyc * (2 * B) + 2 * (b + 1))
                        if b >= 1:
                            pe.wait_ge(h2_ready, cyc * B + b)
                        for kk in range(2):
                            last = nc.tensor.matmul(bank[4][:, :], W.cn_w2[:, kk, :], h1[b % 2][:, kk, :],
                                                    start=kk == 0, stop=kk == 1)
                        last.then_inc(w2_done, 1)
                    if 0 <= k - 2 < B:
                        b = k - 2
                        pe.wait_ge(h2_ready, cyc * B + (b + 1))
                        if b >= 1:
                            pe.wait_ge(h3_ready, cyc * B + b)
                        nc.tensor.matmul(bank[5][0:64, :], W.cn_w3[:, :], h2[b % 2][:, :], start=True,
                                         stop=True).then_inc(w3_done, 1)
                    if 0 <= k - 3 < B:
                        b = k - 3
                        pe.wait_ge(h3_ready, cyc * B + (b + 1))
                        pe.wait_ge(tf_ready, cyc * B + (b + 1))
                        nc.tensor.matmul(bank[6][:, :], W.cn_w4r[:, :], h3[b % 2][:, :], start=True,
                                         stop=True).then_inc(w4_done, 1)
            for b in range(B):
                pe.wait_ge(upd_done, CYCLES * B + b + 1)
                for k in range(2):
                    u = 2 * b + k
                    if u >= 4:
                        pe.wait_ge(x_added, u - 3)
                    for t in range(2):
                        for half in range(2):
                            tok = (2 * k + t) * P
                            last = nc.tensor.transpose(bank[u % 4][:, t * D + half * P:t * D + (half + 1) * P],
                                                       ST[:, half, b, tok:tok + P], W.ident[:, :])
                    last.then_inc(back_turned, 1)

        @block.scalar
        def _(act):
            act.sem_inc(state_in, 4)
            act.sem_inc(tf_ready, 1)
            with act.Fori(0, B // 2) as r:
                for s in range(2):
                    act.wait_ge(xn_turned, r * 2 + s + 3)
                    for half in range(2):
                        nc.scalar.activation(ST[:, half, bass.ds(r * 2 + s, 1), :], bank[2 * s + half][:, :],
                                             ACT.Identity,
                                             accum_out=xsum[:, half, bass.ds(r * 2 + s, 1)]).then_inc(state_in, 1)
            for i, (dst, rows, src, w_bias, scale, func) in enumerate((
                    (g1, P, bank[4], W.gc_b1, 1.0 / N, ACT.Gelu),
                    (g2, 64, bank[5], W.gc_b2, 1.0, ACT.Gelu),
                    (gth, P, bank[6], W.gc_b3h, 0.5, ACT.Tanh))):
                act.wait_ge(g_mm, i + 1)
                nc.scalar.activation(dst[0:rows, :], src[0:rows, 0:B], func, bias=w_bias[0:rows, 0:1],
                                     scale=scale).then_inc(g_act, 1)
            with act.Fori(0, CYCLES) as cyc:
                for k in range(B + SKEW):
                    if k < B:
                        b = k
                        if b >= 2:
                            act.wait_ge(w2_done, cyc * B + (b - 1))
                        for m in range(2):
                            act.wait_ge(w1_done, cyc * (2 * B) + (2 * b + m + 1))
                            nc.scalar.activation(h1[b % 2][:, m, :], bank[2 * (b % 2) + m][:, :], ACT.Gelu,
                                                 bias=W.cn_b1[:, m:m + 1]).then_inc(h1_ready, 1)
                    if 0 <= k - 1 < B:
                        b = k - 1
                        if b >= 2:
                            act.wait_ge(w3_done, cyc * B + (b - 1))
                        act.wait_ge(w2_done, cyc * B + (b + 1))
                        nc.scalar.activation(h2[b % 2][:, :], bank[4][:, :], ACT.Gelu,
                                             bias=W.cn_b2[:, 0:1]).then_inc(h2_ready, 1)
                    if 0 <= k - 2 < B:
                        b = k - 2
                        if b >= 2:
                            act.wait_ge(w4_done, cyc * B + (b - 1))
                        act.wait_ge(w3_done, cyc * B + (b + 1))
                        nc.scalar.activation(h3[b % 2][:, :], bank[5][0:64, :], ACT.Gelu,
                                             bias=W.cn_b3[0:64, 0:1]).then_inc(h3_ready, 1)
                    if 0 <= k - 3 < B:
                        b = k - 3
                        act.wait_ge(upd_done, cyc * B + (B + b - 1))
                        act.wait_ge(w4_done, cyc * B + (b + 1))
                        nc.scalar.activation(tf[b % 2][:, :], bank[6][:, :], ACT.Tanh, bias=W.cn_b4h[:, 0:1],
                                             scale=0.5).then_inc(tf_ready, 1)


class Weights:
    pass


def place_weights(nc, ctx, W):
    def sb(name, shape):
        return ctx.enter_context(nc.sbuf_tensor(name, shape, F32))

    W.cn_w1 = sb("cn_w1", [P, 2, 256])
    W.cn_w2 = sb("cn_w2", [P, 2, P])
    W.cn_w3 = sb("cn_w3", [P, 64])
    W.cn_w4r = sb("cn_w4r", [64, P])
    W.cn_b1 = sb("cn_b1", [P, 2])
    W.cn_b2 = sb("cn_b2", [P, 1])
    W.cn_b3 = sb("cn_b3", [64, 1])
    W.cn_b4h = sb("cn_b4h", [P, 1])
    W.gc_w1 = sb("gc_w1", [P, 2, P])
    W.gc_w2 = sb("gc_w2", [P, 64])
    W.gc_w3r = sb("gc_w3r", [64, P])
    W.gc_b1 = sb("gc_b1", [P, 1])
    W.gc_b2 = sb("gc_b2", [64, 1])
    W.gc_b3h = sb("gc_b3h", [P, 1])
    W.sgn_ar07 = sb("sgn_ar07", [P, 1])
    W.sgn_ar03 = sb("sgn_ar03", [P, 1])
    W.sgn01 = sb("sgn01", [P, 1])
    W.ident = sb("ident", [P, P])
    W.neghalf = sb("neghalf", [P, 32])
    W.Wo = sb("Wo", [P, PAIRS, D])
    W.bgh = sb("bgh", [P, PAIRS])
    W.mixpre = sb("mixpre", [P, P])
    W.mixpost = sb("mixpost", [P, P])
    W.diagmask = sb("diagmask", [P, IG])
    W.memkT = sb("memkT", [P, H, MEM])


def setup_phase(nc, W, X, a, x1_dram):
    with ExitStack() as c:
        def tmp(name, shape):
            return c.enter_context(nc.sbuf_tensor(name, shape, F32))

        def sem(name):
            return c.enter_context(nc.semaphore(name))

        ones = tmp("ones", [P, P])
        zero_tile = tmp("zero_tile", [P, D])
        w4c, g3c, b4c, g3b, arc = (tmp(n, [P, 1]) for n in ("w4c", "g3c", "b4c", "g3b", "arc"))
        sgn = tmp("sgn", [P, 1])
        bgc = tmp("bgc", [P, PAIRS])
        hsc = tmp("hsc", [P, PAIRS])
        wpre = tmp("wpre", [P, H])
        wpost = tmp("wpost", [P, H])
        own = tmp("own", [P, IG])
        iota = tmp("iota", [P, IG])
        row = tmp("row", [P, 1])
        rowi = tmp("rowi", [P, IG])
        mk = tmp("mk", [H * MEM, 2, DH])
        mk2 = tmp("mk2", [H * MEM, DH])
        mss = tmp("mss", [H * MEM, 1])
        mrn = tmp("mrn", [H * MEM, 1])
        turned = c.enter_context(nc.psum_tensor("turned", [P, H * MEM], F32))
        loaded = sem("loaded")
        x_loaded = sem("x_loaded")
        zeroed = sem("zeroed")
        made = sem("made")
        built = sem("built")
        mk_ss = sem("mk_ss")
        mk_rn = sem("mk_rn")
        mk_n = sem("mk_n")
        mk_t = sem("mk_t")
        block = c.enter_context(nc.Block())
        loads = [
            (W.cn_w1[:, :, :], a["cn_w1"].rearrange("(k p) n -> p k n", p=P)),
            (W.cn_w2[:, :, :], a["cn_w2"].rearrange("(k p) n -> p k n", p=P)),
            (W.cn_w3[:, :], a["cn_w3"]),
            (w4c[0:64, :], a["cn_w4"]),
            (W.cn_b1[:, :], a["cn_b1"].rearrange("(m p) -> p m", p=P)),
            (W.cn_b2[:, :], a["cn_b2"].rearrange("(p o) -> p o", o=1)),
            (W.cn_b3[:, :], a["cn_b3"].rearrange("(p o) -> p o", o=1)),
            (b4c[:, :], bcast(a["cn_b4"], [[0, P], [1, 1]])),
            (W.gc_w1[:, :, :], a["gc_w1"].rearrange("(k p) n -> p k n", p=P)),
            (W.gc_w2[:, :], a["gc_w2"]),
            (g3c[0:64, :], a["gc_w3"]),
            (W.gc_b1[:, :], a["gc_b1"].rearrange("(p o) -> p o", o=1)),
            (W.gc_b2[:, :], a["gc_b2"].rearrange("(p o) -> p o", o=1)),
            (g3b[:, :], bcast(a["gc_b3"], [[0, P], [1, 1]])),
            (arc[:, :], bcast(a["adaptive_range"], [[0, P], [1, 1]])),
            (W.Wo[:, :, :], a["Wo"].rearrange("(q p) n -> p q n", p=P)),
            (bgc[:, :], a["bg"].rearrange("(q p) -> p q", p=P)),
            (hsc[0:64, :], bcast(a["head_scale"], [[0, 64], [2, PAIRS]])),
            (hsc[64:128, :], bcast(a["head_scale"], [[0, 64], [2, PAIRS]], 1)),
            (mk[:, 0, :], a["mem_k"].rearrange("h m d -> (h m) d")),
            (mk[:, 1, :], a["mem_k"].rearrange("h m d -> (h m) d")),
        ]
        for g in range(H):
            loads.append((wpre[IG * g:IG * g + IG, :], bcast(a["W_pre_th"], [[0, IG], [H, H]], g)))
            loads.append((wpost[IG * g:IG * g + IG, :], bcast(a["W_post_th"], [[0, IG], [H, H]], g)))

        @block.sync
        def _(sp):
            with nc.allow_non_contiguous_dma("small constants, once"):
                for dst, src in loads:
                    sp.dma_start(dst, src).then_inc(loaded, 16)

        @block.scalar
        def _(act):
            for b in range(B):
                act.dma_start(X[:, b * TPB:(b + 1) * TPB, :], tiles_of(a["x"], b)).then_inc(x_loaded, 16)
            act.wait_ge(zeroed, 1)
            act.dma_start(x1_dram[TILES * P:(TILES + 1) * P, :], zero_tile[:, :]).then_inc(x_loaded, 16)
            act.wait_ge(x_loaded, 16 * (B + 1))

        @block.gpsimd
        def _(pool):
            made_n = 0

            def link(ins):
                ins.then_inc(made, 1)
                nonlocal made_n
                made_n += 1
                pool.wait_ge(made, made_n)

            link(nc.gpsimd.memset(ones[:, :], 1.0))
            link(nc.gpsimd.memset(W.neghalf[:, :], -0.5))
            link(nc.gpsimd.memset(sgn[0:64, :], 1.0))
            link(nc.gpsimd.memset(sgn[64:128, :], -1.0))
            nc.gpsimd.memset(zero_tile[:, :], 0.0).then_inc(zeroed, 1)
            pool.wait_ge(zeroed, 1)
            for i in range(IG):
                link(nc.gpsimd.memset(iota[:, i:i + 1], float(i)))
            link(nc.gpsimd.memset(W.ident[:, :], 0.0))
            link(nc.gpsimd.affine_select(out=W.ident[:, :], in_=W.ident[:, :], compare_op=ALU.not_equal,
                                         fill=1.0, base=0, pattern=[[-1, P]], channel_multiplier=1))
            pool.wait_ge(mk_ss, 1)
            nc.gpsimd.tensor_tensor(mrn[:, :], mss[:, :], W.neghalf[0:H * MEM, 0:1], ALU.pow).then_inc(mk_rn, 1)

        @block.vector
        def _(dve):
            done = [0]

            def link(ins):
                ins.then_inc(built, 1)
                done[0] += 1
                dve.wait_ge(built, done[0])

            dve.wait_ge(loaded, 16 * len(loads))
            dve.wait_ge(made, IG + 6)
            tt, ts = nc.vector.tensor_tensor, nc.vector.tensor_scalar
            link(tt(mk2[:, :], mk[:, 0, :], mk[:, 0, :], ALU.mult))
            link(nc.vector.reduce_sum(mss[:, :], mk2[:, :], axis=AX.X))
            ts(mss[:, :], mss[:, :], 1e-24, None, ALU.max).then_inc(mk_ss, 1)
            link(ts(W.cn_w4r[:, :], ones[0:64, :], w4c[0:64, 0:1], None, ALU.mult))
            link(ts(W.gc_w3r[:, :], ones[0:64, :], g3c[0:64, 0:1], None, ALU.mult))
            link(ts(W.cn_b4h[:, :], b4c[:, :], 0.5, None, ALU.mult))
            link(ts(W.gc_b3h[:, :], g3b[:, :], 0.5, None, ALU.mult))
            link(ts(W.bgh[:, :], bgc[:, :], 0.5, None, ALU.mult))
            link(ts(W.sgn01[:, :], sgn[:, :], 0.1, None, ALU.mult))
            link(tt(arc[:, :], arc[:, :], sgn[:, :], ALU.mult))
            link(ts(W.sgn_ar07[:, :], arc[:, :], 0.7, None, ALU.mult))
            link(ts(W.sgn_ar03[:, :], arc[:, :], 0.3, None, ALU.mult))
            link(nc.vector.reduce_sum(own[:, :], W.ident[:, :].rearrange("p (k i) -> p i k", i=IG), axis=AX.X))
            link(tt(rowi[:, :], own[:, :], iota[:, :], ALU.mult))
            link(nc.vector.reduce_sum(row[:, :], rowi[:, :], axis=AX.X))
            link(ts(W.diagmask[:, :], iota[:, :], row[:, 0:1], -FMAX, ALU.is_gt, ALU.mult))
            link(ts(wpre[:, :], wpre[:, :], QK_SCALE, None, ALU.mult))
            for w, m in ((wpre, W.mixpre), (wpost, W.mixpost)):
                for h in range(H):
                    last = ts(m[:, h * IG:(h + 1) * IG], own[:, :], w[:, h:h + 1], None, ALU.mult)
                link(last)
            link(ts(hsc[:, :], hsc[:, :], 0.5, None, ALU.mult))
            for q in range(PAIRS):
                last = ts(W.Wo[:, q, :], W.Wo[:, q, :], hsc[:, q:q + 1], None, ALU.mult)
            link(last)
            dve.wait_ge(mk_rn, 1)
            ts(mk[:, :, :], mk[:, :, :], mrn[:, 0:1], None, ALU.mult).then_inc(mk_n, 1)
            dve.wait_ge(mk_t, 1)
            link(nc.vector.tensor_copy(W.memkT[:, :, :], turned[:, :].rearrange("p (h m) -> p h m", m=MEM)))

        @block.tensor
        def _(pe):
            pe.wait_ge(mk_n, 1)
            nc.tensor.transpose(turned[:, :], mk[:, :, :].rearrange("p a d -> p (a d)"),
                                W.ident[0:H * MEM, 0:H * MEM]).then_inc(mk_t, 1)


def group_width(n):
    return n * IG + IG + MEM


def attention_phase(nc, W, a, x_dram, out_dram):
    with ExitStack() as c:
        def sb(name, shape):
            return c.enter_context(nc.sbuf_tensor(name, shape, F32))

        Wq, Wk, Wv, Wg = (sb(n, [P, 2, HD]) for n in ("Wq", "Wk", "Wv", "Wg"))
        KT = sb("KT", [P, PAIRS, J])
        V = sb("V", [P, TPB + 1, HD])
        KTnext = sb("KTnext", [P, PAIRS, P])
        Vnext = sb("Vnext", [P, HD])
        xnT = [sb(f"xnT{i}", [P, 2, MEM + P]) for i in range(2)]
        Q = [sb(f"Q{i}", [P, GPT, PAIRS, 32]) for i in range(2)]
        gate = [sb(f"gate{i}", [P, PAIRS, P]) for i in range(2)]
        xt = [sb(f"xt{i}", [P, D]) for i in range(TPB)]
        xn = sb("xn", [P, D])
        stats = sb("stats", [P, 6])
        mv = sb("mv", [P, 2])
        rstd = sb("rstd", [P, 1])
        qk = sb("qk", [P, 2, HD])
        qksq = sb("qksq", [P, HD])
        ssq = sb("ssq", [P, 2, H])
        rn = sb("rn", [P, 2, H])
        raw = [sb(f"raw{i}", [P, J]) for i in range(2)]
        S = [sb(f"S{i}", [P, J]) for i in range(4)]
        work = [sb(f"work{i}", [P, J]) for i in range(2)]
        top = [sb(f"top{i}", [P, TOPK]) for i in range(4)]
        nmax = sb("nmax", [P, 4])
        E = [sb(f"E{i}", [P, (TPB + 1) * P]) for i in range(4)]
        rsum = sb("rsum", [P, 4])
        rinv = sb("rinv", [P, 4])
        R = [sb(f"R{i}", [P, P]) for i in range(4)]
        PT = sb("PT", [P, TPB + 1, H, P // 2])
        oT = sb("oT", [P, PAIRS, P])

        def bank(name):
            return c.enter_context(nc.psum_tensor(name, [P, 512], F32))

        bankA = bank("bankA")
        bankB = [bank(f"bankB{i}") for i in range(2)]
        bankC = [bank(f"bankC{i}") for i in range(2)]
        bankD = [bank(f"bankD{i}") for i in range(2)]
        bankM = bank("bankM")

        LASTG = GPB - 1
        assert group_width(LASTG) - 512 == MEM and group_width(LASTG - 1) <= 512

        with nc.semaphore("w_loaded") as w_loaded, nc.semaphore("zeroed") as zeroed, \
                nc.semaphore("kmem") as kmem, nc.Block() as block:
            @block.sync
            def _(sp):
                for w, src in ((Wq, a["Wq"]), (Wk, a["Wk"]), (Wv, a["Wv"]), (Wg, a["Wg"])):
                    sp.dma_start(w[:, :, :], src.rearrange("(k p) n -> p k n", p=P)).then_inc(w_loaded, 16)
                sp.wait_ge(w_loaded, 64)

            @block.gpsimd
            def _(pool):
                nc.gpsimd.memset(Q[0][:, :, :, :], 0.0).then_inc(zeroed, 1)
                pool.wait_ge(zeroed, 1)
                nc.gpsimd.memset(Q[1][:, :, :, :], 0.0).then_inc(zeroed, 1)

            @block.vector
            def _(dve):
                mk = W.memkT[:, :, :].rearrange("p (q a) m -> p q a m", a=2)
                nc.vector.tensor_copy(KT[0:64, :, 0:MEM], mk[0:64, :, 0, :]).then_inc(kmem, 1)
                nc.vector.tensor_copy(KT[64:128, :, 0:MEM], mk[64:128, :, 1, :]).then_inc(kmem, 1)

        numbers = []

        def body(first, b):
            with ExitStack() as cs:
                def sem(name):
                    s = cs.enter_context(nc.semaphore(name))
                    if not first:
                        numbers.append(s.num)
                    return s

                scored = sem("scored")
                raw_out = sem("raw_out")
                mixed = sem("mixed")
                S_out = sem("S_out")
                masked = sem("masked")
                top_first = sem("top_first")
                nmax_ready = sem("nmax_ready")
                exp_done = sem("exp_done")
                tail_zero = sem("tail_zero")
                E_ready = sem("E_ready")
                R_ready = sem("R_ready")
                turned = sem("turned")
                PT_out = sem("PT_out")
                PT_zero = sem("PT_zero")
                attended = sem("attended")
                gated = sem("gated")
                projected = sem("projected")
                x_added = sem("x_added")
                x_in = [sem(f"x_in{i}") for i in range(TPB)]
                x_out = sem("x_out")
                mv_in = sem("mv_in")
                tk = sem("tk")
                xn_stats = sem("xn_stats")
                xn_rstd = sem("xn_rstd")
                xn_ready = sem("xn_ready")
                D_full = sem("D_full")
                D_read = [sem(f"D{i}_read") for i in range(2)]
                sq_done = sem("sq_done")
                ssq_done = sem("ssq_done")
                rn_ready = sem("rn_ready")
                qk_ready = sem("qk_ready")
                halo = sem("halo")
                moved = sem("moved")
                block = cs.enter_context(nc.Block())

                tiles = [TPB] if first else [1, 2, 3, TPB]
                D_uses = []
                for j in range(len(tiles)):
                    for step in ("xT", "q0", "q1", "k0", "k1", "v0", "v1", "g0", "g1") + \
                            (("w0", "w1") if tiles[j] == TPB - 1 else ()) + ("qT0", "qT1", "kT0", "kT1"):
                        D_uses.append((j, step))

                def D_bank(j, step):
                    return 0 if step == "xT" else int(step[-1])

                def D_index(j, step):
                    i = D_uses.index((j, step))
                    k = D_bank(j, step)
                    return i, sum(D_bank(*u) == k for u in D_uses[:i])

                def pe_use(pe, j, step, emit):
                    i, k = D_index(j, step)
                    d = D_bank(j, step)
                    if k:
                        pe.wait_ge(D_read[d], k)
                    emit(bankD[d]).then_inc(D_full, 1)

                def act_use(act, j, step, emit, also=None):
                    i, k = D_index(j, step)
                    d = D_bank(j, step)
                    act.wait_ge(D_full, i + 1)
                    if also:
                        also(bankD[d])
                    emit(bankD[d]).then_inc(D_read[d], 1)

                def wait_read(eng, j, *steps):
                    for step in steps:
                        eng.wait_ge(D_read[D_bank(j, step)], D_index(j, step)[1] + 1)

                def xtile(j):
                    return xt[tiles[j] % TPB]

                def tpar(j):
                    return tiles[j] % 2

                def dve_ln_stats(dve, j):
                    if j:
                        dve.wait_ge(xn_ready, j)
                    dve.wait_ge(x_in[tiles[j] % TPB], 16)
                    chain(dve, nc.vector.bn_stats(out=stats[:, :], in_=xtile(j)[:, :]))
                    nc.vector.bn_aggr(out=mv[:, :], in_=stats[:, :]).then_inc(tk, 1)
                    chain.n += 1
                    dve.wait_ge(tk, chain.n)
                    nc.vector.tensor_scalar(mv[:, 1:2], mv[:, 1:2], LN_EPS, None, ALU.add).then_inc(xn_stats, 1)

                def dve_ln_apply(dve, j):
                    dve.wait_ge(xn_rstd, j + 1)
                    if j:
                        dve.wait_ge(D_full, D_index(j - 1, "xT")[0] + 1)
                    nc.vector.tensor_scalar(xn[:, :], xtile(j)[:, :], mv[:, 0:1], rstd[:, 0:1],
                                            ALU.subtract, ALU.mult).then_inc(xn_ready, 1)

                def dve_ssq(dve, j, i):
                    dve.wait_ge(sq_done, 2 * j + i + 1)
                    if j:
                        dve.wait_ge(rn_ready, 2 * (j - 1) + i + 1)
                    chain(dve, nc.vector.reduce_sum(ssq[:, i, :], qksq[:, :].rearrange("p (h d) -> p h d", d=DH),
                                                    axis=AX.X))
                    nc.vector.tensor_scalar(ssq[:, i, :], ssq[:, i, :], 1e-24, None, ALU.max).then_inc(ssq_done, 1)

                def pool_rstd(pool, j):
                    pool.wait_ge(xn_stats, j + 1)
                    nc.gpsimd.tensor_tensor(rstd[:, :], mv[:, 1:2], W.neghalf[:, 0:1], ALU.pow).then_inc(xn_rstd, 1)

                def pool_halo(pool, j):
                    dst = xnT[tpar(j)][:, :, 0:MEM]
                    if tiles[j] == TPB:
                        nc.gpsimd.memset(dst, 0.0).then_inc(halo, 1)
                    elif not first and tiles[j] == 1:
                        nc.gpsimd.tensor_copy(dst, xnT[0][:, :, P:P + MEM]).then_inc(halo, 1)
                    else:
                        wait_read(pool, j - 1, "xT")
                        nc.gpsimd.tensor_copy(dst, xnT[1 - tpar(j)][:, :, P:P + MEM]).then_inc(halo, 1)

                def pool_norm(pool, j, i):
                    pool.wait_ge(ssq_done, 2 * j + i + 1)
                    nc.gpsimd.tensor_tensor(rn[:, i, :], ssq[:, i, :], W.neghalf[:, 0:H], ALU.pow).then_inc(rn_ready, 1)
                    pool.wait_ge(rn_ready, 2 * j + i + 1)
                    wait_read(pool, j, f"{'qk'[i]}0", f"{'qk'[i]}1")
                    v = qk[:, i, :].rearrange("p (h d) -> p h d", d=DH)
                    nc.gpsimd.tensor_tensor(v, v, rn[:, i, :].unsqueeze(2).to_broadcast([P, H, DH]),
                                            ALU.mult).then_inc(qk_ready, 1)

                def pe_xT(pe, j):
                    pe.wait_ge(xn_ready, j + 1)

                    def emit(d):
                        for k in range(2):
                            last = nc.tensor.transpose(d[:, k * P:(k + 1) * P], xn[:, k * P:(k + 1) * P], W.ident[:, :])
                        return last
                    pe_use(pe, j, "xT", emit)

                def pe_tokens(pe, j, what, w, cols=slice(MEM, MEM + P), rows=P):
                    wait_read(pe, j, "xT")
                    if what in "vw":
                        pe.wait_ge(halo, j + 1)
                    x = xnT[tpar(j)]
                    for half in range(2):
                        def emit(d):
                            for k in range(2):
                                last = nc.tensor.matmul(d[0:rows, :], x[:, k, cols], w[:, k, half * 512:half * 512 + 512],
                                                        start=k == 0, stop=k == 1)
                            return last
                        pe_use(pe, j, f"{what}{half}", emit)

                def pe_gates(pe, j):
                    x = xnT[tpar(j)]
                    for half in range(2):
                        def emit(d):
                            for q in range(4):
                                for k in range(2):
                                    col = (4 * half + q) * P
                                    last = nc.tensor.matmul(d[:, q * P:(q + 1) * P], Wg[:, k, col:col + P],
                                                            x[:, k, MEM:MEM + P], start=k == 0, stop=k == 1)
                            return last
                        pe_use(pe, j, f"g{half}", emit)

                def pe_turn(pe, j, i, what):
                    pe.wait_ge(qk_ready, 2 * j + i + 1)
                    for half in range(2):
                        def emit(d):
                            for q in range(4):
                                col = (2 * q + half) * P
                                last = nc.tensor.transpose(d[:, q * P:(q + 1) * P], qk[:, i, col:col + P], W.ident[:, :])
                            return last
                        pe_use(pe, j, f"{what}{half}", emit)

                def act_xT(act, j):
                    if j:
                        act.wait_ge(D_full, D_index(j - 1, "g1")[0] + 1)
                    act_use(act, j, "xT", lambda d: nc.scalar.copy(
                        xnT[tpar(j)][:, :, MEM:MEM + P], d[:, 0:D].rearrange("p (k n) -> p k n", k=2)))

                def act_qk(act, j, i, what):
                    if j:
                        act.wait_ge(D_full, D_index(j - 1, f"{'qk'[i]}T1")[0] + 1)
                    if 2 * j + i:
                        act.wait_ge(ssq_done, 2 * j + i)
                    for half in range(2):
                        cols = slice(half * 512, half * 512 + 512)

                        def square(d):
                            ins = nc.scalar.activation(qksq[:, cols], d[:, :], ACT.Square)
                            if half:
                                ins.then_inc(sq_done, 1)
                        act_use(act, j, f"{what}{half}",
                                lambda d: nc.scalar.copy(qk[:, i, cols], d[:, :]), square)

                def act_v(act, j, what, rows=P):
                    t = tiles[j] + (what == "w")
                    for half in range(2):
                        cols = slice(half * 512, half * 512 + 512)
                        dst = Vnext[:, cols] if t == TPB and what == "v" else V[0:rows, t, cols]
                        act_use(act, j, f"{what}{half}",
                                lambda d: nc.scalar.copy(dst, d[0:rows, :]))

                def act_gates(act, j):
                    for half in range(2):
                        def emit(d):
                            for q in range(4):
                                pair = 4 * half + q
                                last = nc.scalar.activation(gate[tpar(j)][:, pair, :], d[:, q * P:(q + 1) * P],
                                                            ACT.Tanh, bias=W.bgh[:, pair:pair + 1], scale=0.5)
                            return last
                        act_use(act, j, f"g{half}", emit)

                def act_qT(act, j):
                    if not first:
                        n = (tiles[j] - 1) * GPT
                        if n:
                            act.wait_ge(scored, n)
                    for half in range(2):
                        def emit(d):
                            for lo in range(2):
                                rows = slice(64 * lo, 64 * lo + 64)
                                slot = (2 * half + lo) * IG
                                dst = Q[tpar(j)][rows, :, half::2, slot:slot + IG].rearrange("p g q i -> p q g i")
                                last = nc.scalar.copy(dst, d[rows, :].rearrange("p (q g i) -> p q g i", q=4, i=IG))
                            return last
                        act_use(act, j, f"qT{half}", emit)

                def act_kT(act, j):
                    t = tiles[j]
                    dst = KTnext[:, :, :] if t == TPB else KT[:, :, MEM + t * P:MEM + (t + 1) * P]
                    for half in range(2):
                        act_use(act, j, f"kT{half}", lambda d: nc.scalar.copy(
                            dst[:, half::2, :], d[:, :].rearrange("p (q n) -> p q n", q=4)))

                def chain(dve, ins):
                    ins.then_inc(tk, 1)
                    chain.n += 1
                    dve.wait_ge(tk, chain.n)
                chain.n = 0

                def sync_memory(sp, j):
                    wait_read(sp, j, "v0", "v1")
                    sp.dma_start(Vnext[0:MEM, :].rearrange("m (h d) -> m h d", d=DH),
                                 a["mem_v"].rearrange("h m d -> m h d")).then_inc(mv_in, 16)
                    sp.wait_ge(mv_in, 16)

                if first:
                    @block.sync
                    def _(sp):
                        sp.dma_start(xt[0][:, :], x_dram[0:P, :]).then_inc(x_in[0], 16)
                        sync_memory(sp, 0)

                    @block.vector
                    def _(dve):
                        dve_ln_stats(dve, 0)
                        dve_ln_apply(dve, 0)
                        dve_ssq(dve, 0, 0)
                        dve_ssq(dve, 0, 1)

                    @block.gpsimd
                    def _(pool):
                        pool_halo(pool, 0)
                        pool_rstd(pool, 0)
                        pool_norm(pool, 0, 0)
                        pool_norm(pool, 0, 1)

                    @block.tensor
                    def _(pe):
                        pe_xT(pe, 0)
                        pe_tokens(pe, 0, "q", Wq)
                        pe_tokens(pe, 0, "k", Wk)
                        pe_tokens(pe, 0, "v", Wv, slice(0, P))
                        pe_gates(pe, 0)
                        pe_turn(pe, 0, 0, "qT")
                        pe_turn(pe, 0, 1, "kT")

                    @block.scalar
                    def _(act):
                        act_xT(act, 0)
                        act_qk(act, 0, 0, "q")
                        act_qk(act, 0, 1, "k")
                        act_v(act, 0, "v")
                        act_gates(act, 0)
                        act_qT(act, 0)
                        act_kT(act, 0)
                    return

                def wide(n):
                    return min(group_width(n), 512)

                def tile_of(n):
                    return n // GPT

                def pe_scores(pe, n):
                    t, g = divmod(n, GPT)
                    if n == 0:
                        pe.wait_ge(moved, 2)
                    elif g == 0:
                        wait_read(pe, t - 1, "kT0", "kT1")
                    if n:
                        pe.wait_ge(raw_out, n)
                    for q in range(2):
                        for grp in range(4):
                            pair = 2 * grp + q
                            last = nc.tensor.matmul(bankA[32 * grp:32 * grp + 32, 0:wide(n)], Q[t % 2][:, g, pair, :],
                                                    KT[:, pair, 0:wide(n)], start=q == 0, stop=q == 1,
                                                    skip_group_check=True)
                    if n == LASTG:
                        pe.wait_ge(gated, 2 * (TPB - 1) + 1)
                        for q in range(2):
                            for grp in range(4):
                                pair = 2 * grp + q
                                last = nc.tensor.matmul(bankM[32 * grp:32 * grp + 32, 0:MEM], Q[t % 2][:, g, pair, :],
                                                        KT[:, pair, 512:J], start=q == 0, stop=q == 1,
                                                        skip_group_check=True)
                    last.then_inc(scored, 1)

                def pe_mix(pe, n):
                    pe.wait_ge(raw_out, n + 1)
                    if n >= 2:
                        pe.wait_ge(S_out, n - 1)
                    last = nc.tensor.matmul(bankB[n % 2][:, 0:wide(n)], W.mixpre[:, :], raw[n % 2][:, 0:wide(n)],
                                            start=True, stop=True)
                    if n == LASTG:
                        last = nc.tensor.matmul(bankM[:, MEM:2 * MEM], W.mixpre[:, :], raw[n % 2][:, 512:J],
                                                start=True, stop=True)
                    last.then_inc(mixed, 1)

                def pe_turn_group(pe, n):
                    t, g = divmod(n, GPT)
                    pe.wait_ge(R_ready, n + 1)
                    pe.wait_ge(tail_zero, n + 1)
                    if n >= 2:
                        pe.wait_ge(PT_out, n - 1)
                    for jb in range(t + 1):
                        last = nc.tensor.matmul(bankC[n % 2][:, jb * P:(jb + 1) * P], E[n % 4][:, jb * P:(jb + 1) * P],
                                                R[n % 4][:, :], start=True, stop=True)
                    if g == GPT - 1:
                        if n == LASTG:
                            pe.wait_ge(S_out, n + 1)
                        else:
                            pe.wait_ge(gated, 2 * t + 1)
                        last = nc.tensor.matmul(bankM[0:MEM, 0:P], E[n % 4][:, (t + 1) * P:(t + 1) * P + MEM],
                                                R[n % 4][:, :], start=True, stop=True)
                    last.then_inc(turned, 1)

                def pe_attend(pe, t, half):
                    pe.wait_ge(PT_out, t * GPT + (half + 1) * (GPT // 2))
                    if t == 0 and half == 0:
                        pe.wait_ge(moved, 4)
                    if half and t == TPB - 1:
                        wait_read(pe, t - 1, "w0", "w1")
                    elif half:
                        wait_read(pe, t, "v0", "v1")
                    if half:
                        pe.wait_ge(PT_zero, t + 1)
                    elif t:
                        pe.wait_ge(x_added, t)
                    blocks = [(jb, P) for jb in range(t + 1)] + ([(t + 1, MEM)] if half else [])
                    for pair in range(PAIRS):
                        for i, (jb, rows) in enumerate(blocks):
                            for lo in range(2):
                                h = 2 * pair + lo
                                last = nc.tensor.matmul(bankM[64 * lo:64 * lo + 64, pair * 64:pair * 64 + 64],
                                                        V[0:rows, jb, h * DH:(h + 1) * DH], PT[0:rows, jb, h, :],
                                                        start=i == 0, stop=i == len(blocks) - 1,
                                                        skip_group_check=True)
                    last.then_inc(attended, 1)

                def pe_project(pe, t):
                    pe.wait_ge(gated, 2 * t + 2)
                    for q in range(PAIRS):
                        last = nc.tensor.matmul(bankM[:, 0:D], oT[:, q, :], W.Wo[:, q, :], start=q == 0,
                                                stop=q == PAIRS - 1)
                    last.then_inc(projected, 1)

                @block.tensor
                def _(pe):
                    for n in range(GPB + LAG):
                        t, g = divmod(n, GPT)
                        if n < GPB:
                            pe_scores(pe, n)
                        if n >= LAG:
                            pe_turn_group(pe, n - LAG)
                        if n < GPB:
                            pe_mix(pe, n)
                        if g == 3 and t:
                            pe_attend(pe, t - 1, 1)
                        if g == 6 and t:
                            pe_project(pe, t - 1)
                        if g == 11:
                            pe_attend(pe, t, 0)
                        if n < GPB:
                            if g == 8:
                                pe_xT(pe, t)
                            if g == 9:
                                pe_tokens(pe, t, "q", Wq)
                            if g == 10:
                                pe_tokens(pe, t, "k", Wk)
                            if g == 11:
                                pe_tokens(pe, t, "v", Wv, slice(0, P))
                            if g == 12:
                                pe_gates(pe, t)
                            if g == 12 and t == TPB - 2:
                                pe_tokens(pe, t, "w", Wv, slice(P, P + MEM), MEM)
                            if g == 13:
                                pe_turn(pe, t, 0, "qT")
                            if g == 14:
                                pe_turn(pe, t, 1, "kT")
                    pe_project(pe, TPB - 1)

                def act_raw(act, n):
                    act.wait_ge(scored, n + 1)
                    if n >= 2:
                        act.wait_ge(mixed, n - 1)
                    last = nc.scalar.copy(raw[n % 2][:, 0:wide(n)], bankA[:, 0:wide(n)])
                    if n == LASTG:
                        last = nc.scalar.copy(raw[n % 2][:, 512:J], bankM[:, 0:MEM])
                    last.then_inc(raw_out, 1)

                def act_S(act, n):
                    act.wait_ge(mixed, n + 1)
                    if n >= 4:
                        act.wait_ge(E_ready, n - 3)
                    last = nc.scalar.copy(S[n % 4][:, 0:wide(n)], bankB[n % 2][:, 0:wide(n)])
                    if n == LASTG:
                        last = nc.scalar.copy(S[n % 4][:, 512:J], bankM[:, MEM:2 * MEM])
                    last.then_inc(S_out, 1)

                def act_exp(act, n):
                    act.wait_ge(nmax_ready, n + 1)
                    w = group_width(n)
                    if n >= 4:
                        act.wait_ge(turned, n - 3)
                    nc.scalar.activation(E[n % 4][:, 0:w], S[n % 4][:, 0:w], ACT.Exp,
                                         bias=nmax[:, n % 4:n % 4 + 1]).then_inc(exp_done, 1)

                def act_PT(act, n):
                    t, g = divmod(n, GPT)
                    half, gh = divmod(g, GPT // 2)
                    act.wait_ge(turned, n + 1)
                    if gh == 0 and n:
                        act.wait_ge(attended, 2 * t + half)
                    last = nc.scalar.copy(PT[:, 0:t + 1, :, gh * IG:(gh + 1) * IG],
                                          bankC[n % 2][:, 0:(t + 1) * P].rearrange("p (j h i) -> p j h i", h=H, i=IG))
                    if g == GPT - 1:
                        act.wait_ge(PT_zero, t + 1)
                        last = nc.scalar.copy(PT[0:MEM, t + 1, :, gh * IG:(gh + 1) * IG],
                                              bankM[0:MEM, 0:P].rearrange("p (h i) -> p h i", i=IG))
                    last.then_inc(PT_out, 1)

                @block.scalar
                def _(act):
                    for n in range(GPB + LAG):
                        t, g = divmod(n, GPT)
                        if n < GPB:
                            act_raw(act, n)
                        if n >= LAG:
                            act_PT(act, n - LAG)
                        if n < GPB:
                            act_S(act, n)
                        if 0 <= n - 2 < GPB:
                            act_exp(act, n - 2)
                        if n < GPB:
                            if g == 8:
                                act_xT(act, t)
                            if g == 9:
                                act_qk(act, t, 0, "q")
                            if g == 10:
                                act_qk(act, t, 1, "k")
                            if g == 11:
                                act_v(act, t, "v")
                            if g == 12:
                                act_gates(act, t)
                            if g == 12 and t == TPB - 2:
                                act_v(act, t, "w", MEM)
                            if g == 13:
                                act_qT(act, t)
                            if g == 14:
                                act_kT(act, t)

                @block.gpsimd
                def _(pool):
                    nc.gpsimd.tensor_copy(KT[:, 0:4, MEM:MEM + P], KTnext[:, 0:4, :]).then_inc(moved, 1)
                    nc.gpsimd.tensor_copy(KT[:, 4:8, MEM:MEM + P], KTnext[:, 4:8, :]).then_inc(moved, 1)
                    pool.wait_ge(moved, 2)
                    nc.gpsimd.tensor_copy(V[:, 0, 0:512], Vnext[:, 0:512]).then_inc(moved, 1)
                    nc.gpsimd.tensor_copy(V[:, 0, 512:HD], Vnext[:, 512:HD]).then_inc(moved, 1)
                    for n in range(GPB + LAG):
                        t, g = divmod(n, GPT)
                        if n >= LAG:
                            m = n - LAG
                            pool.wait_ge(E_ready, m + 1)
                            if m >= 4:
                                pool.wait_ge(turned, m - 3)
                            nc.gpsimd.tensor_scalar(R[m % 4][:, :], W.mixpost[:, :], rinv[:, m % 4:m % 4 + 1], 1.0,
                                                    ALU.mult, ALU.mult).then_inc(R_ready, 1)
                        if n < GPB:
                            lo, hi = group_width(n), (t + 1) * P
                            if n >= 4:
                                pool.wait_ge(turned, n - 3)
                            if lo < hi:
                                nc.gpsimd.memset(E[n % 4][:, lo:hi], 0.0).then_inc(tail_zero, 1)
                            else:
                                pool.sem_inc(tail_zero, 1)
                            pool.wait_ge(S_out, n + 1)
                            w = group_width(n)
                            nc.gpsimd.tensor_tensor(S[n % 4][:, w - IG:w], S[n % 4][:, w - IG:w], W.diagmask[:, :],
                                                    ALU.add).then_inc(masked, 1)
                        if 0 <= n - 2 < GPB:
                            m = n - 2
                            pool.wait_ge(top_first, m + 1)
                            nc.gpsimd.tensor_scalar(nmax[:, m % 4:m % 4 + 1], top[m % 4][:, 0:1], -1.0, 1.0,
                                                    ALU.mult, ALU.mult).then_inc(nmax_ready, 1)
                        if n < GPB:
                            if g == 4:
                                pool_rstd(pool, t)
                            if g == 5:
                                pool_halo(pool, t)
                            if g == 6:
                                if t:
                                    pool.wait_ge(attended, 2 * t)
                                nc.gpsimd.memset(PT[0:MEM, t + 1, :, 0:P // 2 - IG], 0.0).then_inc(PT_zero, 1)
                            if g == 10:
                                pool_norm(pool, t, 0)
                            if g == 12:
                                pool_norm(pool, t, 1)

                @block.sync
                def _(sp):
                    for t in range(1, TPB):
                        sp.dma_start(xt[t][:, :], x_dram[bass.ds(b * N + t * P, P), :]).then_inc(x_in[t], 16)
                    for t in range(TPB):
                        sp.wait_ge(x_added, t + 1)
                        sp.dma_start(out_dram[bass.ds(b * N + t * P, P), :], xt[t][:, :]).then_inc(x_out, 16)
                        if t == 0:
                            sp.wait_ge(x_out, 16)
                            sp.dma_start(xt[0][:, :], x_dram[bass.ds(b * N + N, P), :]).then_inc(x_in[0], 16)
                        if t == TPB - 2:
                            sync_memory(sp, TPB - 1)
                    sp.wait_ge(x_out, 16 * TPB)

                @block.vector
                def _(dve):
                    def gate_rows(t, half):
                        dve.wait_ge(attended, 2 * t + half + 1)
                        if t:
                            dve.wait_ge(projected, t)
                        rows = slice(half * 64, half * 64 + 64)
                        nc.vector.scalar_tensor_tensor(
                            out=oT[:, :, rows], in0=gate[t % 2][:, :, rows], scalar=1.0,
                            in1=bankM[:, :].rearrange("p (q i) -> p q i", q=PAIRS), op0=ALU.add,
                            op1=ALU.mult).then_inc(gated, 1)

                    def residual(t):
                        dve.wait_ge(projected, t + 1)
                        x = xt[t][:, :]
                        nc.vector.tensor_tensor(x, x, bankM[:, 0:D], ALU.add).then_inc(x_added, 1)

                    def top_pair(n0):
                        dep = {}
                        for r in range(TOPK // 8):
                            for n in (n0, n0 + 1):
                                w = group_width(n)
                                if r and w <= TOPK:
                                    continue
                                if r == 0:
                                    dve.wait_ge(masked, n + 1)
                                    if n >= 4:
                                        dve.wait_ge(exp_done, n - 3)
                                else:
                                    dve.wait_ge(tk, dep[n])
                                src = S[n % 4] if r == 0 else work[n % 2]
                                ins = nc.vector.max(top[n % 4][:, 8 * r:8 * r + 8], src[:, 0:w])
                                if r == 0:
                                    ins.then_inc(top_first, 1)
                                    dep[n] = None
                                else:
                                    ins.then_inc(tk, 1)
                                    chain.n += 1
                                    dep[n] = chain.n
                            if r < TOPK // 8 - 1:
                                for n in (n0, n0 + 1):
                                    w = group_width(n)
                                    if w <= TOPK:
                                        continue
                                    if dep[n] is None:
                                        dve.wait_ge(top_first, n + 1)
                                    else:
                                        dve.wait_ge(tk, dep[n])
                                    src = S[n % 4] if r == 0 else work[n % 2]
                                    nc.vector.match_replace(out=work[n % 2][:, 0:w],
                                                            in_to_replace=top[n % 4][:, 8 * r:8 * r + 8],
                                                            in_values=src[:, 0:w], imm_value=-FMAX).then_inc(tk, 1)
                                    chain.n += 1
                                    dep[n] = chain.n
                        for n in (n0, n0 + 1):
                            w = group_width(n)
                            dve.wait_ge(exp_done, n + 1)
                            if dep[n] is not None:
                                dve.wait_ge(tk, dep[n])
                            if n >= 4:
                                dve.wait_ge(R_ready, n - 3)
                            kth = -FMAX if w <= TOPK else top[n % 4][:, TOPK - 1:TOPK]
                            nc.vector.scalar_tensor_tensor(out=E[n % 4][:, 0:w], in0=S[n % 4][:, 0:w], scalar=kth,
                                                           in1=E[n % 4][:, 0:w], op0=ALU.is_ge, op1=ALU.mult,
                                                           accum_out=rsum[:, n % 4:n % 4 + 1]).then_inc(tk, 1)
                            chain.n += 1
                            dep[n] = chain.n
                        for n in (n0, n0 + 1):
                            dve.wait_ge(tk, dep[n])
                            nc.vector.reciprocal(rinv[:, n % 4:n % 4 + 1], rsum[:, n % 4:n % 4 + 1]).then_inc(E_ready, 1)

                    chain.n = 0
                    for n0 in range(0, GPB, 2):
                        t, g = divmod(n0, GPT)
                        top_pair(n0)
                        if g == 0:
                            dve_ln_stats(dve, t)
                        if g == 2 and t:
                            gate_rows(t - 1, 1)
                        if g == 4:
                            dve_ln_apply(dve, t)
                        if g == 6:
                            if t:
                                residual(t - 1)
                            dve_ssq(dve, t, 0)
                        if g == 8:
                            dve_ssq(dve, t, 1)
                        if g == 10:
                            gate_rows(t, 0)
                    gate_rows(TPB - 1, 1)
                    residual(TPB - 1)

        body(True, 0)
        with nc.Fori(0, B) as b:
            body(False, b)
            with nc.Block() as block:
                @block.gpsimd
                def _(pool):
                    pool.sem_clear(range(min(numbers), max(numbers) + 1))


def bcast(ap, pattern, offset=0):
    return bass.AP(tensor=ap.tensor, offset=ap.offset + offset, ap=pattern)


def build(nc, a, out):
    x1_dram = nc.dram_tensor("x1", ((TILES + 1) * P, D), F32, kind="Internal").ap()
    x2_dram = nc.dram_tensor("x2", (TILES * P, D), F32, kind="Internal").ap()
    rows = "b n d -> (b n) d"
    with ExitStack() as ctx:
        W = Weights()
        place_weights(nc, ctx, W)
        with nc.sbuf_tensor("X_first", [P, TILES, D], F32) as X:
            setup_phase(nc, W, X, {**a, "x": a["x"].rearrange(rows)}, x1_dram)
            ffn_phase(nc, "ffn1", X, W, None, x1_dram)
        attention_phase(nc, W, a, x1_dram, x2_dram)
        with nc.sbuf_tensor("X_last", [P, TILES, D], F32) as X:
            ffn_phase(nc, "ffn2", X, W, x2_dram, out.rearrange(rows))


NAMES = {'x': 'L0_attn_x', 'Wq': 'L0_attn_Wq', 'Wk': 'L0_attn_Wk', 'Wv': 'L0_attn_Wv', 'Wg': 'L0_attn_Wg',
         'bg': 'L0_attn_bg', 'Wo': 'L0_attn_Wo', 'W_pre_th': 'L0_attn_W_pre_th',
         'W_post_th': 'L0_attn_W_post_th', 'mem_k': 'L0_attn_mem_k', 'mem_v': 'L0_attn_mem_v',
         'head_scale': 'L0_attn_head_scale_params', 'adaptive_range': 'L0_ffn_adaptive_range',
         **{f'cn_{k}{i}': f'L0_ffn_cn_{k}{i}' for k in 'wb' for i in (1, 2, 3, 4)},
         **{f'gc_{k}{i}': f'L0_ffn_gc_{k}{i}' for k in 'wb' for i in (1, 2, 3)}}


class Inputs:
    pass


def kernel(**inputs):
    import numpy as _np
    import concourse.bacc as _bacc
    from concourse import mybir as _mybir
    from concourse.bass_utils import run_bass_kernel_spmd as _run

    nc = _bacc.Bacc("TRN2", target_bir_lowering=False, num_devices=1)
    arrays, aps = {}, {}
    for short, name in NAMES.items():
        arr = _np.ascontiguousarray(inputs[name])
        arrays[f"in_{name}_dram"] = arr
        aps[short] = nc.dram_tensor(f"in_{name}_dram", arr.shape, _mybir.dt.from_np(arr.dtype),
                                    kind="ExternalInput").ap()
    out = nc.dram_tensor("out_0_dram", (B, N, D), _mybir.dt.float32, kind="ExternalOutput").ap()
    build(nc, aps, out)
    r = _run(nc, [arrays], core_ids=[0])
    return r.results[0]["out_0_dram"]
```

```python
import concourse.bass as bass
from concourse import mybir
import math
from contextlib import ExitStack

F32 = mybir.dt.float32
ALU = mybir.AluOpType
ACT = mybir.ActivationFunctionType
AX = mybir.AxisListType

B, N, D = 8, 512, 256
H, DH, MEM, TOPK = 16, 64, 4, 64
CYCLES = 3
P = 128
TPB = N // P
TILES = B * TPB
IG = 8
GPT = P // IG
GPB = N // IG
PAIRS = H // 2
HD = H * DH
J = N + MEM
SBUFS = 6
LAG = 4
FMAX = float(3.4028234663852886e38)
LN_EPS = 1e-5
QK_SCALE = 10.0

DOWN = 2.0 ** -40
WINDOW = 32
TARGET = 47.5
ROUND = 1.5 * 2.0 ** 23
SUMSQ_LIMIT = 2.0 ** -24
FIRST_TOP = TOPK // IG - 1


def normal_quantile(p):
    lo, hi = -9.0, 9.0
    for _ in range(60):
        mid = (lo + hi) / 2
        lo, hi = (mid, hi) if 0.5 * (1 + math.erf(mid / math.sqrt(2))) < p else (lo, mid)
    return lo


def tiles_of(dram, b):
    return dram[b * N:(b + 1) * N, :].rearrange("(t p) d -> p t d", p=P)


def ffn_phase(nc, tag, X, W, x_dram, out_dram, ahead=()):
    with ExitStack() as c:
        def sb(name, shape):
            return c.enter_context(nc.sbuf_tensor(f"{tag}_{name}", shape, F32))

        def sem(name):
            return c.enter_context(nc.semaphore(f"{tag}_{name}"))

        xn = [sb(f"xn{i}", [P, TPB, D]) for i in range(2)]
        stats = sb("stats", [P, 2, TPB, 6])
        mv = sb("mv", [P, 2, TPB, 2])
        rstd = sb("rstd", [P, 2, TPB])
        ST = sb("state", [P, 2, B, N])
        xsum = sb("xsum", [P, 2, B])
        g1 = sb("g1", [P, B])
        g2 = sb("g2", [64, B])
        gth = sb("gth", [P, B])
        offs = sb("offs", [P, B])
        h1 = [sb(f"h1_{i}", [P, 2, N]) for i in range(2)]
        h2 = [sb(f"h2_{i}", [P, N]) for i in range(2)]
        h3 = [sb(f"h3_{i}", [64, N]) for i in range(2)]
        tf = [sb(f"tf{i}", [P, N]) for i in range(2)]
        cs = sb("cs", [P, N])
        mo = sb("mo", [P, N])
        mp = sb("mp", [P, N])
        bank = [c.enter_context(nc.psum_tensor(f"{tag}_bank{i}", [P, 512], F32)) for i in range(8)]

        x_loaded = [sem(f"x_loaded{i}") for i in range(2)]
        ahead_in = sem("ahead_in")
        stats_ready = sem("stats_ready")
        rstd_ready = sem("rstd_ready")
        xn_ready = sem("xn_ready")
        xn_turned = sem("xn_turned")
        state_in = sem("state_in")
        g_mm = sem("g_mm")
        g_act = sem("g_act")
        offs_ready = sem("offs_ready")
        w1_done, w2_done, w3_done, w4_done = (sem(f"w{i}_done") for i in (1, 2, 3, 4))
        h1_ready, h2_ready, h3_ready, tf_ready = (sem(n) for n in ("h1_ready", "h2_ready", "h3_ready", "tf_ready"))
        waited = sem("waited")
        vec = sem("vec")
        upd_done = sem("upd_done")
        back_turned = sem("back_turned")
        x_added = sem("x_added")
        stored = sem("stored")

        block = c.enter_context(nc.Block())
        SKEW = 3

        @block.sync
        def _(sp):
            if x_dram is not None:
                for b in range(B):
                    sp.dma_start(X[:, b * TPB:(b + 1) * TPB, :], tiles_of(x_dram, b)).then_inc(x_loaded[2 * b // B], 16)
            for dst, src in ahead:
                sp.dma_start(dst, src).then_inc(ahead_in, 16)
            for b in range(B):
                sp.wait_ge(x_added, 2 * (b + 1))
                sp.dma_start(tiles_of(out_dram, b), X[:, b * TPB:(b + 1) * TPB, :]).then_inc(stored, 16)
            sp.wait_ge(stored, 16 * B)
            if ahead:
                sp.wait_ge(ahead_in, 16 * len(ahead))

        @block.vector
        def _(dve):
            dve.sem_inc(upd_done, B)
            for part in range(2):
                if x_dram is not None:
                    dve.wait_ge(x_loaded[part], 16 * (B // 2))
                with dve.Fori(part * (B // 4), (part + 1) * (B // 4)) as r:
                    for s in range(2):
                        for t in range(TPB):
                            nc.vector.bn_stats(out=stats[:, s, t, :],
                                               in_=X[:, bass.ds(r * (2 * TPB) + (s * TPB + t), 1), :]).then_inc(vec, 1)
                        dve.wait_ge(vec, r * 16 + 8 * s + 4)
                        dve.sem_inc(waited, 1)
                        for t in range(TPB):
                            last = nc.vector.bn_aggr(out=mv[:, s, t, :], in_=stats[:, s, t, :])
                            last.then_inc(vec, 1)
                        dve.wait_ge(vec, r * 16 + 8 * s + 8)
                        nc.vector.tensor_scalar(mv[:, s, :, 1], mv[:, s, :, 1], LN_EPS, None,
                                                ALU.add).then_inc(stats_ready, 1)
                        dve.wait_ge(rstd_ready, r * 2 + s + 1)
                        dve.wait_ge(xn_turned, r * 2 + s + 1)
                        for t in range(TPB):
                            last = nc.vector.tensor_scalar(
                                xn[s][:, t, :], X[:, bass.ds(r * (2 * TPB) + (s * TPB + t), 1), :],
                                mv[:, s, t, 0:1], rstd[:, s, t:t + 1], ALU.subtract, ALU.mult)
                        last.then_inc(xn_ready, 1)
                        dve.wait_ge(xn_ready, r * 2 + s + 1)
            dve.wait_ge(g_act, 3)
            nc.vector.tensor_scalar(offs[:, :], gth[:, :], W.sgn_ar07[:, 0:1], W.sgn01[:, 0:1], ALU.mult,
                                    ALU.add).then_inc(offs_ready, 1)
            dve.wait_ge(offs_ready, 1)
            with dve.Fori(0, CYCLES) as cyc:
                for b in range(B):
                    at = cyc * (4 * B) + (8 * B + 4 * b)
                    o, p = ST[:, 0, b, :], ST[:, 1, b, :]
                    dve.wait_ge(tf_ready, cyc * B + (b + 2))
                    dve.wait_ge(vec, at)
                    dve.wait_ge(upd_done, cyc * B + (B + b))
                    nc.vector.tensor_scalar(cs[:, :], tf[b % 2][:, :], W.sgn_ar03[:, 0:1], offs[:, b:b + 1],
                                            ALU.mult, ALU.add).then_inc(vec, 1)
                    dve.wait_ge(vec, at + 1)
                    nc.vector.tensor_tensor(mo[:, :], cs[:, :], p, ALU.mult).then_inc(vec, 1)
                    nc.vector.tensor_tensor(mp[:, :], cs[:, :], o, ALU.mult).then_inc(vec, 1)
                    dve.wait_ge(vec, at + 3)
                    nc.vector.tensor_tensor(o, o, mo[:, :], ALU.add).then_inc(vec, 1)
                    nc.vector.tensor_tensor(p, p, mp[:, :], ALU.subtract).then_inc(upd_done, 1)
            for b in range(B):
                for k in range(2):
                    u = 2 * b + k
                    dve.wait_ge(back_turned, u + 1)
                    xt = X[:, b * TPB + 2 * k:b * TPB + 2 * k + 2, :]
                    nc.vector.scalar_tensor_tensor(out=xt, in0=bank[u % 4].rearrange("p (t d) -> p t d", t=2),
                                                   scalar=0.5, in1=xt, op0=ALU.mult,
                                                   op1=ALU.add).then_inc(x_added, 1)

        @block.gpsimd
        def _(pool):
            with pool.Fori(0, B // 2) as r:
                for s in range(2):
                    pool.wait_ge(stats_ready, r * 2 + s + 1)
                    nc.gpsimd.tensor_tensor(rstd[:, s, :], mv[:, s, :, 1], W.neghalf[:, 0:TPB],
                                            ALU.pow).then_inc(rstd_ready, 1)

        @block.tensor
        def _(pe):
            pe.sem_inc(xn_turned, 2)
            with pe.Fori(0, B // 2) as r:
                for s in range(2):
                    pe.wait_ge(xn_ready, r * 2 + s + 1)
                    pe.wait_ge(state_in, r * 4 + (2 * s + 2))
                    for half in range(2):
                        for t in range(TPB):
                            last = nc.tensor.transpose(bank[2 * s + half][:, t * P:(t + 1) * P],
                                                       xn[s][:, t, half * P:(half + 1) * P], W.ident[:, :])
                    last.then_inc(xn_turned, 1)
            pe.wait_ge(state_in, 4 + 2 * B)
            for k in range(2):
                last = nc.tensor.matmul(bank[4][:, 0:B], W.gc_w1[:, k, :], xsum[:, k, :], start=k == 0, stop=k == 1)
            last.then_inc(g_mm, 1)
            pe.wait_ge(g_act, 1)
            nc.tensor.matmul(bank[5][0:64, 0:B], W.gc_w2[:, :], g1[:, :], start=True, stop=True).then_inc(g_mm, 1)
            pe.wait_ge(g_act, 2)
            nc.tensor.matmul(bank[6][:, 0:B], W.gc_w3r[:, :], g2[:, :], start=True, stop=True).then_inc(g_mm, 1)
            pe.wait_ge(g_act, 3)

            with pe.Fori(0, CYCLES) as cyc:
                for k in range(B + SKEW):
                    if k < B:
                        b = k
                        if b >= 2:
                            pe.wait_ge(h1_ready, cyc * (2 * B) + 2 * (b - 1))
                        pe.wait_ge(upd_done, cyc * B + (b + 1))
                        for m in range(2):
                            for kk in range(2):
                                last = nc.tensor.matmul(bank[2 * (b % 2) + m][:, :],
                                                        W.cn_w1[:, kk, m * P:(m + 1) * P], ST[:, kk, b, :],
                                                        start=kk == 0, stop=kk == 1)
                            last.then_inc(w1_done, 1)
                    if 0 <= k - 1 < B:
                        b = k - 1
                        pe.wait_ge(h1_ready, cyc * (2 * B) + 2 * (b + 1))
                        if b >= 1:
                            pe.wait_ge(h2_ready, cyc * B + b)
                        for kk in range(2):
                            last = nc.tensor.matmul(bank[4][:, :], W.cn_w2[:, kk, :], h1[b % 2][:, kk, :],
                                                    start=kk == 0, stop=kk == 1)
                        last.then_inc(w2_done, 1)
                    if 0 <= k - 2 < B:
                        b = k - 2
                        pe.wait_ge(h2_ready, cyc * B + (b + 1))
                        if b >= 1:
                            pe.wait_ge(h3_ready, cyc * B + b)
                        nc.tensor.matmul(bank[5][0:64, :], W.cn_w3[:, :], h2[b % 2][:, :], start=True,
                                         stop=True).then_inc(w3_done, 1)
                    if 0 <= k - 3 < B:
                        b = k - 3
                        pe.wait_ge(h3_ready, cyc * B + (b + 1))
                        pe.wait_ge(tf_ready, cyc * B + (b + 1))
                        nc.tensor.matmul(bank[6][:, :], W.cn_w4r[:, :], h3[b % 2][:, :], start=True,
                                         stop=True).then_inc(w4_done, 1)
            for b in range(B):
                pe.wait_ge(upd_done, CYCLES * B + b + 1)
                for k in range(2):
                    u = 2 * b + k
                    if u >= 4:
                        pe.wait_ge(x_added, u - 3)
                    for t in range(2):
                        for half in range(2):
                            tok = (2 * k + t) * P
                            last = nc.tensor.transpose(bank[u % 4][:, t * D + half * P:t * D + (half + 1) * P],
                                                       ST[:, half, b, tok:tok + P], W.ident[:, :])
                    last.then_inc(back_turned, 1)

        @block.scalar
        def _(act):
            act.sem_inc(state_in, 4)
            act.sem_inc(tf_ready, 1)
            with act.Fori(0, B // 2) as r:
                for s in range(2):
                    act.wait_ge(xn_turned, r * 2 + s + 3)
                    for half in range(2):
                        nc.scalar.activation(ST[:, half, bass.ds(r * 2 + s, 1), :], bank[2 * s + half][:, :],
                                             ACT.Identity,
                                             accum_out=xsum[:, half, bass.ds(r * 2 + s, 1)]).then_inc(state_in, 1)
            for i, (dst, rows, src, w_bias, scale, func) in enumerate((
                    (g1, P, bank[4], W.gc_b1, 1.0 / N, ACT.Gelu),
                    (g2, 64, bank[5], W.gc_b2, 1.0, ACT.Gelu),
                    (gth, P, bank[6], W.gc_b3h, 0.5, ACT.Tanh))):
                act.wait_ge(g_mm, i + 1)
                nc.scalar.activation(dst[0:rows, :], src[0:rows, 0:B], func, bias=w_bias[0:rows, 0:1],
                                     scale=scale).then_inc(g_act, 1)
            with act.Fori(0, CYCLES) as cyc:
                for k in range(B + SKEW):
                    if k < B:
                        b = k
                        if b >= 2:
                            act.wait_ge(w2_done, cyc * B + (b - 1))
                        for m in range(2):
                            act.wait_ge(w1_done, cyc * (2 * B) + (2 * b + m + 1))
                            nc.scalar.activation(h1[b % 2][:, m, :], bank[2 * (b % 2) + m][:, :], ACT.Gelu,
                                                 bias=W.cn_b1[:, m:m + 1]).then_inc(h1_ready, 1)
                    if 0 <= k - 1 < B:
                        b = k - 1
                        if b >= 2:
                            act.wait_ge(w3_done, cyc * B + (b - 1))
                        act.wait_ge(w2_done, cyc * B + (b + 1))
                        nc.scalar.activation(h2[b % 2][:, :], bank[4][:, :], ACT.Gelu,
                                             bias=W.cn_b2[:, 0:1]).then_inc(h2_ready, 1)
                    if 0 <= k - 2 < B:
                        b = k - 2
                        if b >= 2:
                            act.wait_ge(w4_done, cyc * B + (b - 1))
                        act.wait_ge(w3_done, cyc * B + (b + 1))
                        nc.scalar.activation(h3[b % 2][:, :], bank[5][0:64, :], ACT.Gelu,
                                             bias=W.cn_b3[0:64, 0:1]).then_inc(h3_ready, 1)
                    if 0 <= k - 3 < B:
                        b = k - 3
                        act.wait_ge(upd_done, cyc * B + (B + b - 1))
                        act.wait_ge(w4_done, cyc * B + (b + 1))
                        nc.scalar.activation(tf[b % 2][:, :], bank[6][:, :], ACT.Tanh, bias=W.cn_b4h[:, 0:1],
                                             scale=0.5).then_inc(tf_ready, 1)


class Weights:
    pass


def place_weights(nc, ctx, W):
    def sb(name, shape):
        return ctx.enter_context(nc.sbuf_tensor(name, shape, F32))

    W.cn_w1 = sb("cn_w1", [P, 2, 256])
    W.cn_w2 = sb("cn_w2", [P, 2, P])
    W.cn_w3 = sb("cn_w3", [P, 64])
    W.cn_w4r = sb("cn_w4r", [64, P])
    W.cn_b1 = sb("cn_b1", [P, 2])
    W.cn_b2 = sb("cn_b2", [P, 1])
    W.cn_b3 = sb("cn_b3", [64, 1])
    W.cn_b4h = sb("cn_b4h", [P, 1])
    W.gc_w1 = sb("gc_w1", [P, 2, P])
    W.gc_w2 = sb("gc_w2", [P, 64])
    W.gc_w3r = sb("gc_w3r", [64, P])
    W.gc_b1 = sb("gc_b1", [P, 1])
    W.gc_b2 = sb("gc_b2", [64, 1])
    W.gc_b3h = sb("gc_b3h", [P, 1])
    W.sgn_ar07 = sb("sgn_ar07", [P, 1])
    W.sgn_ar03 = sb("sgn_ar03", [P, 1])
    W.sgn01 = sb("sgn01", [P, 1])
    W.ident = sb("ident", [P, P])
    W.neghalf = sb("neghalf", [P, 32])
    W.Wo = sb("Wo", [P, PAIRS, D])
    W.bgh = sb("bgh", [P, PAIRS])
    W.mixpre = sb("mixpre", [P, P])
    W.mixpost = sb("mixpost", [P, P])
    W.diagmask = sb("diagmask", [P, IG])
    W.diagmask_all = sb("diagmask_all", [P, IG])
    W.half = sb("half", [P, 1])
    W.iotaM = sb("iotaM", [P, WINDOW])
    W.rankM = sb("rankM", [P, 1])
    W.ones = sb("ones", [P, P])
    W.memkT = sb("memkT", [P, H, MEM])


def setup_phase(nc, W, X, a, x1_dram):
    with ExitStack() as c:
        def tmp(name, shape):
            return c.enter_context(nc.sbuf_tensor(name, shape, F32))

        def sem(name):
            return c.enter_context(nc.semaphore(name))

        ones = W.ones
        future = tmp("future", [P, 1])
        zero_tile = tmp("zero_tile", [P, D])
        w4c, g3c, b4c, g3b, arc = (tmp(n, [P, 1]) for n in ("w4c", "g3c", "b4c", "g3b", "arc"))
        sgn = tmp("sgn", [P, 1])
        bgc = tmp("bgc", [P, PAIRS])
        hsc = tmp("hsc", [P, PAIRS])
        wpre = tmp("wpre", [P, H])
        wpost = tmp("wpost", [P, H])
        own = tmp("own", [P, IG])
        iota = tmp("iota", [P, IG])
        row = tmp("row", [P, 1])
        rowi = tmp("rowi", [P, IG])
        mk = tmp("mk", [H * MEM, 2, DH])
        mk2 = tmp("mk2", [H * MEM, DH])
        mss = tmp("mss", [H * MEM, 1])
        mrn = tmp("mrn", [H * MEM, 1])
        turned = c.enter_context(nc.psum_tensor("turned", [P, H * MEM], F32))
        loaded = sem("loaded")
        x_loaded = sem("x_loaded")
        zeroed = sem("zeroed")
        made = sem("made")
        built = sem("built")
        mk_ss = sem("mk_ss")
        mk_rn = sem("mk_rn")
        mk_n = sem("mk_n")
        mk_t = sem("mk_t")
        block = c.enter_context(nc.Block())
        loads = [
            (W.cn_w1[:, :, :], a["cn_w1"].rearrange("(k p) n -> p k n", p=P)),
            (W.cn_w2[:, :, :], a["cn_w2"].rearrange("(k p) n -> p k n", p=P)),
            (W.cn_w3[:, :], a["cn_w3"]),
            (w4c[0:64, :], a["cn_w4"]),
            (W.cn_b1[:, :], a["cn_b1"].rearrange("(m p) -> p m", p=P)),
            (W.cn_b2[:, :], a["cn_b2"].rearrange("(p o) -> p o", o=1)),
            (W.cn_b3[:, :], a["cn_b3"].rearrange("(p o) -> p o", o=1)),
            (b4c[:, :], bcast(a["cn_b4"], [[0, P], [1, 1]])),
            (W.gc_w1[:, :, :], a["gc_w1"].rearrange("(k p) n -> p k n", p=P)),
            (W.gc_w2[:, :], a["gc_w2"]),
            (g3c[0:64, :], a["gc_w3"]),
            (W.gc_b1[:, :], a["gc_b1"].rearrange("(p o) -> p o", o=1)),
            (W.gc_b2[:, :], a["gc_b2"].rearrange("(p o) -> p o", o=1)),
            (g3b[:, :], bcast(a["gc_b3"], [[0, P], [1, 1]])),
            (arc[:, :], bcast(a["adaptive_range"], [[0, P], [1, 1]])),
            (W.Wo[:, :, :], a["Wo"].rearrange("(q p) n -> p q n", p=P)),
            (bgc[:, :], a["bg"].rearrange("(q p) -> p q", p=P)),
            (hsc[0:64, :], bcast(a["head_scale"], [[0, 64], [2, PAIRS]])),
            (hsc[64:128, :], bcast(a["head_scale"], [[0, 64], [2, PAIRS]], 1)),
            (mk[:, 0, :], a["mem_k"].rearrange("h m d -> (h m) d")),
            (mk[:, 1, :], a["mem_k"].rearrange("h m d -> (h m) d")),
        ]
        for g in range(H):
            loads.append((wpre[IG * g:IG * g + IG, :], bcast(a["W_pre_th"], [[0, IG], [H, H]], g)))
            loads.append((wpost[IG * g:IG * g + IG, :], bcast(a["W_post_th"], [[0, IG], [H, H]], g)))

        @block.sync
        def _(sp):
            with nc.allow_non_contiguous_dma("small constants, once"):
                for dst, src in loads:
                    sp.dma_start(dst, src).then_inc(loaded, 16)

        @block.scalar
        def _(act):
            for b in range(B):
                act.dma_start(X[:, b * TPB:(b + 1) * TPB, :], tiles_of(a["x"], b)).then_inc(x_loaded, 16)
            act.wait_ge(zeroed, 1)
            act.dma_start(x1_dram[TILES * P:(TILES + 1) * P, :], zero_tile[:, :]).then_inc(x_loaded, 16)
            act.wait_ge(x_loaded, 16 * (B + 1))

        @block.gpsimd
        def _(pool):
            made_n = 0

            def link(ins):
                ins.then_inc(made, 1)
                nonlocal made_n
                made_n += 1
                pool.wait_ge(made, made_n)

            link(nc.gpsimd.memset(ones[:, :], 1.0))
            link(nc.gpsimd.memset(W.neghalf[:, :], -0.5))
            link(nc.gpsimd.memset(sgn[0:64, :], 1.0))
            link(nc.gpsimd.memset(sgn[64:128, :], -1.0))
            nc.gpsimd.memset(zero_tile[:, :], 0.0).then_inc(zeroed, 1)
            pool.wait_ge(zeroed, 1)
            for i in range(IG):
                link(nc.gpsimd.memset(iota[:, i:i + 1], float(i)))
            for i in range(WINDOW):
                link(nc.gpsimd.memset(W.iotaM[:, i:i + 1], ROUND + i))
            link(nc.gpsimd.memset(W.half[:, :], 0.5))
            link(nc.gpsimd.memset(W.ident[:, :], 0.0))
            link(nc.gpsimd.affine_select(out=W.ident[:, :], in_=W.ident[:, :], compare_op=ALU.not_equal,
                                         fill=1.0, base=0, pattern=[[-1, P]], channel_multiplier=1))
            pool.wait_ge(mk_ss, 1)
            nc.gpsimd.tensor_tensor(mrn[:, :], mss[:, :], W.neghalf[0:H * MEM, 0:1], ALU.pow).then_inc(mk_rn, 1)

        @block.vector
        def _(dve):
            done = [0]

            def link(ins):
                ins.then_inc(built, 1)
                done[0] += 1
                dve.wait_ge(built, done[0])

            dve.wait_ge(loaded, 16 * len(loads))
            dve.wait_ge(made, IG + WINDOW + 7)
            tt, ts = nc.vector.tensor_tensor, nc.vector.tensor_scalar
            link(tt(mk2[:, :], mk[:, 0, :], mk[:, 0, :], ALU.mult))
            link(nc.vector.reduce_sum(mss[:, :], mk2[:, :], axis=AX.X))
            ts(mss[:, :], mss[:, :], 1e-24, None, ALU.max).then_inc(mk_ss, 1)
            link(ts(W.cn_w4r[:, :], ones[0:64, :], w4c[0:64, 0:1], None, ALU.mult))
            link(ts(W.gc_w3r[:, :], ones[0:64, :], g3c[0:64, 0:1], None, ALU.mult))
            link(ts(W.cn_b4h[:, :], b4c[:, :], 0.5, None, ALU.mult))
            link(ts(W.gc_b3h[:, :], g3b[:, :], 0.5, None, ALU.mult))
            link(ts(W.bgh[:, :], bgc[:, :], 0.5, None, ALU.mult))
            link(ts(W.sgn01[:, :], sgn[:, :], 0.1, None, ALU.mult))
            link(tt(arc[:, :], arc[:, :], sgn[:, :], ALU.mult))
            link(ts(W.sgn_ar07[:, :], arc[:, :], 0.7, None, ALU.mult))
            link(ts(W.sgn_ar03[:, :], arc[:, :], 0.3, None, ALU.mult))
            link(nc.vector.reduce_sum(own[:, :], W.ident[:, :].rearrange("p (k i) -> p i k", i=IG), axis=AX.X))
            link(tt(rowi[:, :], own[:, :], iota[:, :], ALU.mult))
            link(nc.vector.reduce_sum(row[:, :], rowi[:, :], axis=AX.X))
            link(ts(W.diagmask[:, :], iota[:, :], row[:, 0:1], -2.0, ALU.is_gt, ALU.mult))
            link(ts(W.diagmask_all[:, :], iota[:, :], row[:, 0:1], -FMAX / 2 * DOWN, ALU.is_gt, ALU.mult))
            link(ts(future[:, :], row[:, :], -2.0, 63.0 + 2.0 * (IG - 1), ALU.mult, ALU.add))
            link(ts(W.rankM[:, :], future[:, :], ROUND, None, ALU.add))
            link(ts(wpre[:, :], wpre[:, :], QK_SCALE, DOWN, ALU.mult, ALU.mult))
            for w, m in ((wpre, W.mixpre), (wpost, W.mixpost)):
                for h in range(H):
                    last = ts(m[:, h * IG:(h + 1) * IG], own[:, :], w[:, h:h + 1], None, ALU.mult)
                link(last)
            link(ts(hsc[:, :], hsc[:, :], 0.5, None, ALU.mult))
            for q in range(PAIRS):
                last = ts(W.Wo[:, q, :], W.Wo[:, q, :], hsc[:, q:q + 1], None, ALU.mult)
            link(last)
            dve.wait_ge(mk_rn, 1)
            ts(mk[:, :, :], mk[:, :, :], mrn[:, 0:1], None, ALU.mult).then_inc(mk_n, 1)
            dve.wait_ge(mk_t, 1)
            link(nc.vector.tensor_copy(W.memkT[:, :, :], turned[:, :].rearrange("p (h m) -> p h m", m=MEM)))

        @block.tensor
        def _(pe):
            pe.wait_ge(mk_n, 1)
            nc.tensor.transpose(turned[:, :], mk[:, :, :].rearrange("p a d -> p (a d)"),
                                W.ident[0:H * MEM, 0:H * MEM]).then_inc(mk_t, 1)


def group_width(n):
    return n * IG + IG + MEM


def attention_phase(nc, W, token_weights, a, x_dram, out_dram):
    with ExitStack() as c:
        def sb(name, shape):
            return c.enter_context(nc.sbuf_tensor(name, shape, F32))

        Wq, Wk, Wv, Wg = token_weights
        KT = sb("KT", [P, PAIRS, J])
        V = sb("V", [P, TPB + 1, HD])
        xnT = [sb(f"xnT{i}", [P, 2, MEM + P]) for i in range(2)]
        Q = sb("Q", [P, GPT, PAIRS, 32])
        gate = [sb(f"gate{i}", [P, PAIRS, P]) for i in range(2)]
        xt = [sb(f"xt{i}", [P, D]) for i in range(TPB)]
        stats = sb("stats", [P, 6])
        mv = sb("mv", [P, 2])
        rstd = sb("rstd", [P, 1])
        qk = sb("qk", [P, 2, HD])
        qksq = sb("qksq", [P, HD])
        xn = qksq[:, 0:D]
        ssq = sb("ssq", [P, 2, H])
        rn = sb("rn", [P, 2, H])
        raw = [sb(f"raw{i}", [P, J]) for i in range(2)]
        S = [sb(f"S{i}", [P, J]) for i in range(SBUFS)]
        lowered = [sb(f"lowered{i}", [P, J]) for i in range(2)]
        work = [sb(f"work{i}", [P, J]) for i in range(2)]
        top = [sb(f"top{i}", [P, TOPK]) for i in range(2)]
        nmax = sb("nmax", [P, 8])
        E = [sb(f"E{i}", [P, J]) for i in range(4)]
        rmax = sb("rmax", [P, 8])
        kth = sb("kth", [P, 8])
        sums = sb("sums", [P, 8])
        sumsq = sb("sumsq", [P, GPB + 1])
        count = sb("count", [P, 8])
        rank = sb("rank", [P, GPB])
        est = sb("est", [P, 8, 4])
        thr = sb("thr", [P, 8])
        picked = [sb(f"picked{i}", [P, WINDOW]) for i in range(2)]
        junk = c.enter_context(nc.sbuf_tensor("junk", [P, J], mybir.dt.bfloat16))
        worst = sb("worst", [P, 2])
        flag = sb("flag", [P, 1])
        again = c.enter_context(nc.sbuf_tensor("again", [P, 1], mybir.dt.int32))
        rsum = sb("rsum", [P, 8])
        rinv = sb("rinv", [P, 8])
        R = [sb(f"R{i}", [P, P]) for i in range(2)]
        PT = sb("PT", [P, TPB + 1, H, P])
        oT = sb("oT", [P, PAIRS, P])

        def bank(name):
            return c.enter_context(nc.psum_tensor(name, [P, 512], F32))

        bankA = bank("bankA")
        bankB = [bank(f"bankB{i}") for i in range(2)]
        bankC = [bank(f"bankC{i}") for i in range(2)]
        bankD = [bank(f"bankD{i}") for i in range(2)]
        bankM = bank("bankM")

        LASTG = GPB - 1
        assert group_width(LASTG) - 512 == MEM and group_width(LASTG - 1) <= 512

        with nc.semaphore("zeroed") as zeroed, \
                nc.semaphore("kmem") as kmem, nc.Block() as block:
            @block.gpsimd
            def _(pool):
                nc.gpsimd.memset(Q[:, :, :, :], 0.0).then_inc(zeroed, 1)

            @block.vector
            def _(dve):
                mk = W.memkT[:, :, :].rearrange("p (q a) m -> p q a m", a=2)
                nc.vector.tensor_copy(KT[0:64, :, 0:MEM], mk[0:64, :, 0, :]).then_inc(kmem, 1)
                nc.vector.tensor_copy(KT[64:128, :, 0:MEM], mk[64:128, :, 1, :]).then_inc(kmem, 1)

        counters = {}

        def body(mode, b):
            first, fast = mode == "first", mode == "fast"
            with ExitStack() as cs:
                def sem(name):
                    if name not in counters:
                        counters[name] = c.enter_context(nc.semaphore(name))
                    return counters[name]

                scored = sem("scored")
                raw_out = sem("raw_out")
                mixed = sem("mixed")
                S_out = sem("S_out")
                masked = sem("masked")
                top_first = sem("top_first")
                nmax_ready = sem("nmax_ready")
                exp_done = sem("exp_done")
                tail_zero = sem("tail_zero")
                E_ready = sem("E_ready")
                R_ready = sem("R_ready")
                turned = sem("turned")
                PT_out = sem("PT_out")
                PT_zero = sem("PT_zero")
                attended = sem("attended")
                gated = sem("gated")
                projected = sem("projected")
                x_added = sem("x_added")
                x_in = [sem(f"x_in{i}") for i in range(TPB)]
                x_out = sem("x_out")
                mv_in = sem("mv_in")
                summed = sem("summed")
                est_chain = sem("est_chain")
                thr_ready = sem("thr_ready")
                lower_done = sem("lower_done")
                count_done = sem("count_done")
                flagged = sem("flagged")
                flag_sum = sem("flag_sum")
                rank_ready = sem("rank_ready")
                picked_done = sem("picked_done")
                tk = sem("tk")
                xn_stats = sem("xn_stats")
                xn_rstd = sem("xn_rstd")
                xn_ready = sem("xn_ready")
                D_full = sem("D_full")
                D_read = [sem(f"D{i}_read") for i in range(2)]
                sq_done = sem("sq_done")
                ssq_done = sem("ssq_done")
                rn_ready = sem("rn_ready")
                qk_ready = sem("qk_ready")
                halo = sem("halo")
                block = cs.enter_context(nc.Block())

                tiles = [TPB] if first else [0, 1, 2, 3, TPB]
                D_uses = []
                for j, t in enumerate(tiles):
                    steps = ["xT", "q0", "q1", "k0", "k1", "v0", "v1", "g0", "g1", "w0", "w1",
                             "qT0", "qT1", "kT0", "kT1"]
                    if t != TPB - 1:
                        steps = [x for x in steps if x[0] != "w"]
                    if t == TPB:
                        steps = [x for x in steps if x[0] != "v"]
                    D_uses += [(j, x) for x in (["v0", "v1"] if t == 0 else steps)]

                def full(j):
                    return j if first else j - 1

                def D_bank(j, step):
                    return 0 if step == "xT" else int(step[-1])

                def D_index(j, step):
                    i = D_uses.index((j, step))
                    k = D_bank(j, step)
                    return i, sum(D_bank(*u) == k for u in D_uses[:i])

                def pe_use(pe, j, step, emit):
                    i, k = D_index(j, step)
                    d = D_bank(j, step)
                    if k:
                        pe.wait_ge(D_read[d], k)
                    emit(bankD[d]).then_inc(D_full, 1)

                def act_use(act, j, step, emit, also=None):
                    i, k = D_index(j, step)
                    d = D_bank(j, step)
                    act.wait_ge(D_full, i + 1)
                    if also:
                        also(bankD[d])
                    emit(bankD[d]).then_inc(D_read[d], 1)

                def wait_read(eng, j, *steps):
                    for step in steps:
                        eng.wait_ge(D_read[D_bank(j, step)], D_index(j, step)[1] + 1)

                def xtile(j):
                    return xt[tiles[j] % TPB]

                def tpar(j):
                    return tiles[j] % 2

                def dve_ln_stats(dve, j):
                    if full(j):
                        dve.wait_ge(xn_ready, full(j))
                    dve.wait_ge(x_in[tiles[j] % TPB], 16)
                    chain(dve, nc.vector.bn_stats(out=stats[:, :], in_=xtile(j)[:, :]))
                    nc.vector.bn_aggr(out=mv[:, :], in_=stats[:, :]).then_inc(tk, 1)
                    chain.n += 1
                    dve.wait_ge(tk, chain.n)
                    nc.vector.tensor_scalar(mv[:, 1:2], mv[:, 1:2], LN_EPS, None, ALU.add).then_inc(xn_stats, 1)

                def dve_ln_apply(dve, j):
                    dve.wait_ge(xn_rstd, full(j) + 1)
                    if full(j):
                        dve.wait_ge(D_full, D_index(j - 1, "xT")[0] + 1)
                    nc.vector.tensor_scalar(xn, xtile(j)[:, :], mv[:, 0:1], rstd[:, 0:1],
                                            ALU.subtract, ALU.mult).then_inc(xn_ready, 1)

                def dve_ssq(dve, j, i):
                    dve.wait_ge(sq_done, 2 * full(j) + i + 1)
                    if full(j):
                        dve.wait_ge(rn_ready, 2 * (full(j) - 1) + i + 1)
                    chain(dve, nc.vector.reduce_sum(ssq[:, i, :], qksq[:, :].rearrange("p (h d) -> p h d", d=DH),
                                                    axis=AX.X))
                    nc.vector.tensor_scalar(ssq[:, i, :], ssq[:, i, :], 1e-24, None, ALU.max).then_inc(ssq_done, 1)

                def pool_rstd(pool, j):
                    pool.wait_ge(xn_stats, full(j) + 1)
                    nc.gpsimd.tensor_tensor(rstd[:, :], mv[:, 1:2], W.neghalf[:, 0:1], ALU.pow).then_inc(xn_rstd, 1)

                def pool_halo(pool, j):
                    dst = xnT[tpar(j)][:, :, 0:MEM]
                    if tiles[j] == TPB:
                        nc.gpsimd.memset(dst, 0.0).then_inc(halo, 1)
                    elif not first and tiles[j] == 1:
                        nc.gpsimd.tensor_copy(dst, xnT[0][:, :, P:P + MEM]).then_inc(halo, 1)
                    else:
                        wait_read(pool, j - 1, "xT")
                        nc.gpsimd.tensor_copy(dst, xnT[1 - tpar(j)][:, :, P:P + MEM]).then_inc(halo, 1)

                def pool_norm(pool, j, i):
                    pool.wait_ge(ssq_done, 2 * full(j) + i + 1)
                    nc.gpsimd.tensor_tensor(rn[:, i, :], ssq[:, i, :], W.neghalf[:, 0:H], ALU.pow).then_inc(rn_ready, 1)
                    pool.wait_ge(rn_ready, 2 * full(j) + i + 1)
                    wait_read(pool, j, f"{'qk'[i]}0", f"{'qk'[i]}1")
                    v = qk[:, i, :].rearrange("p (h d) -> p h d", d=DH)
                    nc.gpsimd.tensor_tensor(v, v, rn[:, i, :].unsqueeze(2).to_broadcast([P, H, DH]),
                                            ALU.mult).then_inc(qk_ready, 1)

                def pe_xT(pe, j):
                    pe.wait_ge(xn_ready, full(j) + 1)
                    if not first and tiles[j] > 1:
                        pe.wait_ge(gated, tiles[j] - 1)

                    def emit(d):
                        for k in range(2):
                            last = nc.tensor.transpose(d[:, k * P:(k + 1) * P], xn[:, k * P:(k + 1) * P], W.ident[:, :])
                        return last
                    pe_use(pe, j, "xT", emit)

                def pe_tokens(pe, j, what, w, cols=slice(MEM, MEM + P), rows=P):
                    if tiles[j]:
                        wait_read(pe, j, "xT")
                        if what in "vw":
                            pe.wait_ge(halo, full(j) + 1)
                    x = xnT[tpar(j)]
                    for half in range(2):
                        def emit(d):
                            for k in range(2):
                                last = nc.tensor.matmul(d[0:rows, :], x[:, k, cols], w[:, k, half * 512:half * 512 + 512],
                                                        start=k == 0, stop=k == 1)
                            return last
                        pe_use(pe, j, f"{what}{half}", emit)

                def pe_gates(pe, j):
                    x = xnT[tpar(j)]
                    for half in range(2):
                        def emit(d):
                            for q in range(4):
                                for k in range(2):
                                    col = (4 * half + q) * P
                                    last = nc.tensor.matmul(d[:, q * P:(q + 1) * P], Wg[:, k, col:col + P],
                                                            x[:, k, MEM:MEM + P], start=k == 0, stop=k == 1)
                            return last
                        pe_use(pe, j, f"g{half}", emit)

                def pe_turn(pe, j, i, what):
                    pe.wait_ge(qk_ready, 2 * full(j) + i + 1)
                    for half in range(2):
                        def emit(d):
                            for q in range(4):
                                col = (2 * q + half) * P
                                last = nc.tensor.transpose(d[:, q * P:(q + 1) * P], qk[:, i, col:col + P], W.ident[:, :])
                            return last
                        pe_use(pe, j, f"{what}{half}", emit)

                def act_xT(act, j):
                    if full(j):
                        act.wait_ge(D_full, D_index(j - 1, "g1")[0] + 1)
                    act_use(act, j, "xT", lambda d: nc.scalar.copy(
                        xnT[tpar(j)][:, :, MEM:MEM + P], d[:, 0:D].rearrange("p (k n) -> p k n", k=2)))

                def act_qk(act, j, i, what):
                    if full(j):
                        act.wait_ge(D_full, D_index(j - 1, f"{'qk'[i]}T1")[0] + 1)
                    if 2 * full(j) + i:
                        act.wait_ge(ssq_done, 2 * full(j) + i)
                    for half in range(2):
                        cols = slice(half * 512, half * 512 + 512)

                        def square(d):
                            ins = nc.scalar.activation(qksq[:, cols], d[:, :], ACT.Square)
                            if half:
                                ins.then_inc(sq_done, 1)
                        act_use(act, j, f"{what}{half}",
                                lambda d: nc.scalar.copy(qk[:, i, cols], d[:, :]), square)

                def act_v(act, j, what, rows=P):
                    t = tiles[j] + (what == "w")
                    for half in range(2):
                        cols = slice(half * 512, half * 512 + 512)
                        dst = V[0:rows, t, cols]
                        act_use(act, j, f"{what}{half}",
                                lambda d: nc.scalar.copy(dst, d[0:rows, :]))

                def act_gates(act, j):
                    for half in range(2):
                        def emit(d):
                            for q in range(4):
                                pair = 4 * half + q
                                last = nc.scalar.activation(gate[tpar(j)][:, pair, :], d[:, q * P:(q + 1) * P],
                                                            ACT.Tanh, bias=W.bgh[:, pair:pair + 1], scale=0.5)
                            return last
                        act_use(act, j, f"g{half}", emit)

                def act_qT(act, j):
                    if not first:
                        act.wait_ge(scored, tiles[j] * GPT)
                    for half in range(2):
                        def emit(d):
                            for lo in range(2):
                                rows = slice(64 * lo, 64 * lo + 64)
                                slot = (2 * half + lo) * IG
                                dst = Q[rows, :, half::2, slot:slot + IG].rearrange("p g q i -> p q g i")
                                last = nc.scalar.copy(dst, d[rows, :].rearrange("p (q g i) -> p q g i", q=4, i=IG))
                            return last
                        act_use(act, j, f"qT{half}", emit)

                def act_kT(act, j):
                    t = tiles[j]
                    if t == TPB:
                        t = 0
                    dst = KT[:, :, MEM + t * P:MEM + (t + 1) * P]
                    for half in range(2):
                        act_use(act, j, f"kT{half}", lambda d: nc.scalar.copy(
                            dst[:, half::2, :], d[:, :].rearrange("p (q n) -> p q n", q=4)))

                def chain(dve, ins):
                    ins.then_inc(tk, 1)
                    chain.n += 1
                    dve.wait_ge(tk, chain.n)
                chain.n = 0

                def sync_memory(sp, j):
                    wait_read(sp, j, "v0", "v1")
                    sp.dma_start(V[0:MEM, 0, :].rearrange("m (h d) -> m h d", d=DH),
                                 a["mem_v"].rearrange("h m d -> m h d")).then_inc(mv_in, 16)
                    sp.wait_ge(mv_in, 16)

                if first:
                    @block.sync
                    def _(sp):
                        sp.dma_start(xt[0][:, :], x_dram[0:P, :] if b is None else x_dram[bass.ds(b * N, P), :]).then_inc(x_in[0], 16)
                        sp.wait_ge(x_in[0], 16)

                    @block.vector
                    def _(dve):
                        dve_ln_stats(dve, 0)
                        dve_ln_apply(dve, 0)
                        dve_ssq(dve, 0, 0)
                        dve_ssq(dve, 0, 1)

                    @block.gpsimd
                    def _(pool):
                        pool_halo(pool, 0)
                        pool_rstd(pool, 0)
                        pool_norm(pool, 0, 0)
                        pool_norm(pool, 0, 1)

                    @block.tensor
                    def _(pe):
                        pe_xT(pe, 0)
                        pe_tokens(pe, 0, "q", Wq)
                        pe_tokens(pe, 0, "k", Wk)
                        pe_gates(pe, 0)
                        pe_turn(pe, 0, 0, "qT")
                        pe_turn(pe, 0, 1, "kT")

                    @block.scalar
                    def _(act):
                        act_xT(act, 0)
                        act_qk(act, 0, 0, "q")
                        act_qk(act, 0, 1, "k")
                        act_gates(act, 0)
                        act_qT(act, 0)
                        act_kT(act, 0)
                    return

                def wide(n):
                    return min(group_width(n), 512)

                def pe_scores(pe, n):
                    t, g = divmod(n, GPT)
                    if g == 0 and t:
                        wait_read(pe, t, "qT0", "qT1", "kT0", "kT1")
                    if n:
                        pe.wait_ge(raw_out, n)
                    for q in range(2):
                        for grp in range(4):
                            pair = 2 * grp + q
                            last = nc.tensor.matmul(bankA[32 * grp:32 * grp + 32, 0:wide(n)], Q[:, g, pair, :],
                                                    KT[:, pair, 0:wide(n)], start=q == 0, stop=q == 1,
                                                    skip_group_check=True)
                    if n == LASTG:
                        pe.wait_ge(x_added, TPB - 1)
                        for q in range(2):
                            for grp in range(4):
                                pair = 2 * grp + q
                                last = nc.tensor.matmul(bankM[32 * grp:32 * grp + 32, 0:MEM], Q[:, g, pair, :],
                                                        KT[:, pair, 512:J], start=q == 0, stop=q == 1,
                                                        skip_group_check=True)
                    last.then_inc(scored, 1)

                def pe_mix(pe, n):
                    pe.wait_ge(raw_out, n + 1)
                    if n >= 2:
                        pe.wait_ge(S_out, n - 1)
                    last = nc.tensor.matmul(bankB[n % 2][:, 0:wide(n)], W.mixpre[:, :], raw[n % 2][:, 0:wide(n)],
                                            start=True, stop=True)
                    if n == LASTG:
                        last = nc.tensor.matmul(bankM[:, MEM:2 * MEM], W.mixpre[:, :], raw[n % 2][:, 512:J],
                                                start=True, stop=True)
                    last.then_inc(mixed, 1)

                def pe_turn_group(pe, n):
                    t, g = divmod(n, GPT)
                    pe.wait_ge(R_ready, n + 1)
                    pe.wait_ge(tail_zero, 4 * t + min(g, 3) + 1)
                    if n >= 2:
                        pe.wait_ge(PT_out, n - 1)
                    for jb in range(t + 1):
                        last = nc.tensor.matmul(bankC[n % 2][:, jb * P:(jb + 1) * P], E[n % 4][:, jb * P:(jb + 1) * P],
                                                R[n % 2][:, :], start=True, stop=True)
                    if g == GPT - 1:
                        if n == LASTG:
                            pe.wait_ge(S_out, n + 1)
                        else:
                            if t:
                                pe.wait_ge(x_added, t)
                        last = nc.tensor.matmul(bankM[0:MEM, 0:P], E[n % 4][:, (t + 1) * P:(t + 1) * P + MEM],
                                                R[n % 2][:, :], start=True, stop=True)
                    last.then_inc(turned, 1)

                def pe_attend(pe, t):
                    pe.wait_ge(PT_out, (t + 1) * GPT)
                    pe.wait_ge(PT_zero, t + 1)
                    if t == 0:
                        pe.wait_ge(mv_in, 16)
                    if t == TPB - 1:
                        wait_read(pe, t, "w0", "w1")
                        wait_read(pe, t + 1, "kT0")
                    else:
                        wait_read(pe, t + 1, "v0", "v1", "kT0")
                    blocks = [(jb, P) for jb in range(t + 1)] + [(t + 1, MEM)]
                    for pair in range(PAIRS):
                        dst = bankM if pair < 4 else bankD[0]
                        for i, (jb, rows) in enumerate(blocks):
                            for lo in range(2):
                                h = 2 * pair + lo
                                last = nc.tensor.matmul(dst[64 * lo:64 * lo + 64, (pair % 4) * P:(pair % 4 + 1) * P],
                                                        V[0:rows, jb, h * DH:(h + 1) * DH], PT[0:rows, jb, h, :],
                                                        start=i == 0, stop=i == len(blocks) - 1,
                                                        skip_group_check=True)
                    last.then_inc(attended, 1)

                def pe_project(pe, t):
                    pe.wait_ge(gated, t + 1)
                    for q in range(PAIRS):
                        last = nc.tensor.matmul(bankM[:, 0:D], oT[:, q, :], W.Wo[:, q, :], start=q == 0,
                                                stop=q == PAIRS - 1)
                    last.then_inc(projected, 1)

                @block.tensor
                def _(pe):
                    pe_scores(pe, 0)
                    for n0 in range(0, GPB + LAG, 2):
                        t, g = divmod(n0, GPT)
                        if n0 < GPB:
                            pe_mix(pe, n0)
                            pe_scores(pe, n0 + 1)
                            if g == 8:
                                pe_xT(pe, t + 1)
                            if g == 10:
                                pe_tokens(pe, t + 1, "k", Wk)
                            if g == 12:
                                pe_gates(pe, t + 1)
                                if t == TPB - 2:
                                    pe_tokens(pe, t + 1, "w", Wv, slice(P, P + MEM), MEM)
                            if g == 14:
                                pe_turn(pe, t + 1, 0, "qT")
                            pe_mix(pe, n0 + 1)
                            if g == 14:
                                pe_turn(pe, t + 1, 1, "kT")
                        if n0 >= LAG:
                            pe_turn_group(pe, n0 - LAG)
                        if g == 6 and t:
                            pe_project(pe, t - 1)
                        if n0 + 2 < GPB:
                            pe_scores(pe, n0 + 2)
                        if n0 >= LAG:
                            pe_turn_group(pe, n0 + 1 - LAG)
                        if g == 2 and t:
                            pe_attend(pe, t - 1)
                        if n0 == 0:
                            pe_tokens(pe, 0, "v", Wv, slice(0, P))
                        if n0 < GPB:
                            if g == 8:
                                pe_tokens(pe, t + 1, "q", Wq)
                            if g == 10 and t < TPB - 1:
                                pe_tokens(pe, t + 1, "v", Wv, slice(0, P))
                    if fast:
                        pe.wait_ge(flagged, 1)
                        nc.tensor.matmul(bankA[:, 0:1], W.ones[:, :], flag[:, :], start=True, stop=True) \
                            .then_inc(flag_sum, 1)
                    pe_project(pe, TPB - 1)

                def act_raw(act, n):
                    act.wait_ge(scored, n + 1)
                    if n >= 2:
                        act.wait_ge(mixed, n - 1)
                    last = nc.scalar.copy(raw[n % 2][:, 0:wide(n)], bankA[:, 0:wide(n)])
                    if n == LASTG:
                        last = nc.scalar.copy(raw[n % 2][:, 512:J], bankM[:, 0:MEM])
                    last.then_inc(raw_out, 1)

                def act_S(act, n):
                    act.wait_ge(mixed, n + 1)
                    if n >= SBUFS:
                        act.wait_ge(E_ready, n - SBUFS + 1)
                    ranked = fast and n >= FIRST_TOP
                    if ranked:
                        if n - 8 >= FIRST_TOP:
                            act.wait_ge(thr_ready, n - 7 - FIRST_TOP)
                        if n > FIRST_TOP:
                            act.wait_ge(summed, n - FIRST_TOP)
                        before = n // 2 * 2 - 2
                        if before > FIRST_TOP:
                            act.wait_ge(count_done, before - FIRST_TOP)
                        nc.scalar.activation(junk[:, 0:wide(n)], bankB[n % 2][:, 0:wide(n)], ACT.Square,
                                             accum_out=sumsq[:, n:n + 1]).then_inc(summed, 1)
                        if n == LASTG:
                            act.wait_ge(summed, n - FIRST_TOP + 1)
                            nc.scalar.activation(junk[:, 0:MEM], bankM[:, MEM:2 * MEM], ACT.Square,
                                                 accum_out=sumsq[:, GPB:GPB + 1]).then_inc(summed, 1)
                            nc.scalar.copy(S[n % SBUFS][:, 512:J], bankM[:, MEM:2 * MEM])
                        nc.scalar.activation(S[n % SBUFS][:, 0:wide(n)], bankB[n % 2][:, 0:wide(n)], ACT.Identity,
                                             accum_out=sums[:, n % 8:n % 8 + 1]).then_inc(S_out, 1)
                        return
                    last = nc.scalar.copy(S[n % SBUFS][:, 0:wide(n)], bankB[n % 2][:, 0:wide(n)])
                    if n == LASTG:
                        last = nc.scalar.copy(S[n % SBUFS][:, 512:J], bankM[:, MEM:2 * MEM])
                    last.then_inc(S_out, 1)

                def act_exp(act, n):
                    act.wait_ge(nmax_ready, n + 1)
                    w = group_width(n)
                    if n >= 4:
                        act.wait_ge(turned, n - 3)
                    nc.scalar.activation(E[n % 4][:, 0:w], S[n % SBUFS][:, 0:w], ACT.Exp,
                                         bias=nmax[:, n % 8:n % 8 + 1], scale=1.0 / DOWN).then_inc(exp_done, 1)

                def act_count(act, n):
                    act.wait_ge(lower_done, n + 1 - FIRST_TOP)
                    before = min(n // 2 * 2 + 4, GPB)
                    act.wait_ge(summed, before - FIRST_TOP + (before == GPB))
                    if n > FIRST_TOP:
                        act.wait_ge(count_done, n - FIRST_TOP)
                    if n - 8 >= FIRST_TOP:
                        act.wait_ge(rank_ready, n - 7 - FIRST_TOP)
                    w = group_width(n)
                    nc.scalar.activation(junk[:, 0:w], lowered[n % 2][:, 0:w], ACT.Identity,
                                         accum_out=count[:, n % 8:n % 8 + 1]).then_inc(count_done, 1)

                def act_PT(act, n):
                    t, g = divmod(n, GPT)
                    act.wait_ge(turned, n + 1)
                    if g == 0 and t:
                        act.wait_ge(attended, t)
                    last = nc.scalar.copy(PT[:, 0:t + 1, :, g * IG:(g + 1) * IG],
                                          bankC[n % 2][:, 0:(t + 1) * P].rearrange("p (j h i) -> p j h i", h=H, i=IG))
                    if g == GPT - 1:
                        act.wait_ge(PT_zero, t + 1)
                        last = nc.scalar.copy(PT[0:MEM, t + 1, :, g * IG:(g + 1) * IG],
                                              bankM[0:MEM, 0:P].rearrange("p (h i) -> p h i", i=IG))
                    last.then_inc(PT_out, 1)

                @block.scalar
                def _(act):
                    act_raw(act, 0)
                    for n0 in range(0, GPB + LAG, 2):
                        t, g = divmod(n0, GPT)
                        if n0 < GPB:
                            act_S(act, n0)
                            act_raw(act, n0 + 1)
                            if g == 8:
                                act_xT(act, t + 1)
                            if g == 10:
                                act_qk(act, t + 1, 1, "k")
                            if g == 12:
                                act_gates(act, t + 1)
                                if t == TPB - 2:
                                    act_v(act, t + 1, "w", MEM)
                            if g == 14:
                                act_qT(act, t + 1)
                            act_S(act, n0 + 1)
                            if g == 14:
                                act_kT(act, t + 1)
                        if n0 >= 2 and n0 - 2 < GPB:
                            act_exp(act, n0 - 2)
                            act_exp(act, n0 - 1)
                        if n0 >= LAG:
                            act_PT(act, n0 - LAG)
                        if n0 >= 2 and n0 - 2 < GPB:
                            for n in (n0 - 2, n0 - 1):
                                if fast and n >= FIRST_TOP:
                                    act_count(act, n)
                        if n0 + 2 < GPB:
                            act_raw(act, n0 + 2)
                        if n0 >= LAG:
                            act_PT(act, n0 + 1 - LAG)
                        if n0 == 0:
                            act_v(act, 0, "v")
                        if n0 < GPB:
                            if g == 8:
                                act_qk(act, t + 1, 0, "q")
                            if g == 10 and t < TPB - 1:
                                act_v(act, t + 1, "v")

                def pool_threshold(pool, n):
                    k = n % 8
                    step = 4 * (n - FIRST_TOP)
                    visible = n * IG + MEM + (IG + 1) / 2
                    z = normal_quantile(1 - TARGET / visible)
                    inv = 1.0 / wide(n)
                    mean, msq, var, dev = (est[:, k, i:i + 1] for i in range(4))
                    nc.gpsimd.tensor_scalar(msq, sums[:, k:k + 1], sums[:, k:k + 1], inv * inv, ALU.mult, ALU.mult) \
                        .then_inc(est_chain, 1)
                    nc.gpsimd.tensor_scalar(mean, sums[:, k:k + 1], inv, 1.0, ALU.mult, ALU.mult) \
                        .then_inc(est_chain, 1)
                    pool.wait_ge(est_chain, step + 2)
                    nc.gpsimd.tensor_scalar(var, sumsq[:, n:n + 1], inv, msq, ALU.mult, ALU.subtract) \
                        .then_inc(est_chain, 1)
                    pool.wait_ge(est_chain, step + 3)
                    nc.gpsimd.tensor_tensor(dev, var, W.half[:, 0:1], ALU.pow).then_inc(est_chain, 1)
                    pool.wait_ge(est_chain, step + 4)
                    if n - 8 >= FIRST_TOP:
                        pool.wait_ge(lower_done, n - 7 - FIRST_TOP)
                    nc.gpsimd.tensor_scalar(thr[:, k:k + 1], dev, z, mean, ALU.mult, ALU.add) \
                        .then_inc(thr_ready, 1)

                @block.gpsimd
                def _(pool):
                    for n0 in range(0, GPB + LAG, 2):
                        t, g = divmod(n0, GPT)
                        both = (n0, n0 + 1)
                        if n0 >= LAG:
                            for m in (n0 - LAG, n0 + 1 - LAG):
                                pool.wait_ge(E_ready, m + 1)
                                if m >= 2:
                                    pool.wait_ge(turned, m - 1)
                                nc.gpsimd.tensor_scalar(R[m % 2][:, :], W.mixpost[:, :], rinv[:, m % 8:m % 8 + 1],
                                                        1.0, ALU.mult, ALU.mult).then_inc(R_ready, 1)
                        if 0 <= n0 - 2 < GPB:
                            m = n0 - 2
                            cols = slice(m % 8, m % 8 + 2)
                            pool.wait_ge(top_first, m + 2)
                            if m >= 8:
                                pool.wait_ge(exp_done, m - 6)
                            nc.gpsimd.tensor_scalar(nmax[:, cols], rmax[:, cols], -1.0, 1.0 / DOWN, ALU.mult,
                                                    ALU.mult).then_inc(nmax_ready, 2)
                        if n0 >= GPB:
                            continue
                        for n in both:
                            pool.wait_ge(S_out, n + 1)
                            w = group_width(n)
                            mask = W.diagmask if fast else W.diagmask_all
                            nc.gpsimd.tensor_tensor(S[n % SBUFS][:, w - IG:w], S[n % SBUFS][:, w - IG:w], mask[:, :],
                                                    ALU.add).then_inc(masked, 1)
                            if fast and n >= FIRST_TOP:
                                pool_threshold(pool, n)
                        if g < 4:
                            for n in both:
                                if n >= 4:
                                    pool.wait_ge(turned, n - 3)
                                nc.gpsimd.memset(E[n % 4][:, group_width(n):(t + 1) * P], 0.0).then_inc(tail_zero, 1)
                        if g == 4:
                            pool_rstd(pool, t + 1)
                            pool_halo(pool, t + 1)
                        if g == 6:
                            if t:
                                pool.wait_ge(attended, t)
                            nc.gpsimd.memset(PT[0:MEM, t + 1, :, 0:P - IG], 0.0).then_inc(PT_zero, 1)
                        if g == 10:
                            pool_norm(pool, t + 1, 0)
                        if g == 12:
                            pool_norm(pool, t + 1, 1)

                @block.sync
                def _(sp):
                    sync_memory(sp, 0)
                    for t in range(1, TPB):
                        sp.dma_start(xt[t][:, :], x_dram[bass.ds(b * N + t * P, P), :]).then_inc(x_in[t], 16)
                    for t in range(TPB):
                        sp.wait_ge(x_added, t + 1)
                        sp.dma_start(out_dram[bass.ds(b * N + t * P, P), :], xt[t][:, :]).then_inc(x_out, 16)
                        if t == 0:
                            sp.wait_ge(x_out, 16)
                            sp.dma_start(xt[0][:, :], x_dram[bass.ds(b * N + N, P), :]).then_inc(x_in[0], 16)
                    sp.wait_ge(x_out, 16 * TPB)

                @block.vector
                def _(dve):
                    def gate_tile(t):
                        dve.wait_ge(attended, t + 1)
                        if t:
                            dve.wait_ge(projected, t)
                        for half, src in enumerate((bankM, bankD[0])):
                            q = slice(4 * half, 4 * half + 4)
                            last = nc.vector.scalar_tensor_tensor(
                                out=oT[:, q, :], in0=gate[t % 2][:, q, :], scalar=1.0,
                                in1=src[:, :].rearrange("p (q i) -> p q i", q=4), op0=ALU.add, op1=ALU.mult)
                        last.then_inc(gated, 1)

                    def residual(t):
                        dve.wait_ge(projected, t + 1)
                        x = xt[t][:, :]
                        nc.vector.tensor_tensor(x, x, bankM[:, 0:D], ALU.add).then_inc(x_added, 1)

                    def step(ins, n, dep):
                        ins.then_inc(tk, 1)
                        chain.n += 1
                        dep[n] = chain.n

                    def top_pair(n0):
                        both = (n0, n0 + 1)
                        ranked = [n for n in both if n >= FIRST_TOP]
                        dep = {}
                        for n in both:
                            dve.wait_ge(masked, n + 1)
                            if n >= 8:
                                dve.wait_ge(nmax_ready, n - 7)
                            nc.vector.reduce_max(rmax[:, n % 8:n % 8 + 1], S[n % SBUFS][:, 0:group_width(n)],
                                                 axis=AX.X).then_inc(top_first, 1)
                        if fast:
                            for n in ranked:
                                w = group_width(n)
                                dve.wait_ge(thr_ready, n + 1 - FIRST_TOP)
                                if n - 2 >= FIRST_TOP:
                                    dve.wait_ge(count_done, n - 1 - FIRST_TOP)
                                nc.vector.scalar_tensor_tensor(
                                    out=lowered[n % 2][:, 0:w], in0=S[n % SBUFS][:, 0:w],
                                    scalar=thr[:, n % 8:n % 8 + 1], in1=S[n % SBUFS][:, 0:w], op0=ALU.is_ge,
                                    op1=ALU.subtract, reverse1=True).then_inc(lower_done, 1)
                        rounds = (WINDOW if fast else TOPK) // 8
                        for r in range(rounds):
                            for n in ranked:
                                src = work[n % 2] if r else lowered[n % 2] if fast else S[n % SBUFS]
                                if n in dep:
                                    dve.wait_ge(tk, dep[n])
                                elif fast:
                                    dve.wait_ge(lower_done, n + 1 - FIRST_TOP)
                                step(nc.vector.max(top[n % 2][:, 8 * r:8 * r + 8], src[:, 0:group_width(n)]), n, dep)
                            if r < rounds - 1:
                                for n in ranked:
                                    src = work[n % 2] if r else lowered[n % 2] if fast else S[n % SBUFS]
                                    w = group_width(n)
                                    dve.wait_ge(tk, dep[n])
                                    step(nc.vector.match_replace(
                                        out=work[n % 2][:, 0:w], in_to_replace=top[n % 2][:, 8 * r:8 * r + 8],
                                        in_values=src[:, 0:w], imm_value=-FMAX), n, dep)
                        if fast and ranked:
                            cols = slice(ranked[0] % 8, ranked[-1] % 8 + 1)
                            dve.wait_ge(count_done, ranked[-1] + 1 - FIRST_TOP)
                            nc.vector.tensor_scalar(rank[:, ranked[0]:ranked[-1] + 1], count[:, cols],
                                                    W.rankM[:, 0:1], None, ALU.add).then_inc(rank_ready, len(ranked))
                            for n in ranked:
                                dve.wait_ge(rank_ready, n + 1 - FIRST_TOP)
                                dve.wait_ge(tk, dep[n])
                                if n - 2 >= FIRST_TOP:
                                    dve.wait_ge(picked_done, n - 1 - FIRST_TOP)
                                nc.vector.scalar_tensor_tensor(
                                    out=picked[n % 2][:, :], in0=W.iotaM[:, :], scalar=rank[:, n:n + 1],
                                    in1=top[n % 2][:, 0:WINDOW], op0=ALU.is_equal, op1=ALU.mult,
                                    accum_out=kth[:, n % 8:n % 8 + 1]).then_inc(picked_done, 1)
                        for n in both:
                            w = group_width(n)
                            dve.wait_ge(exp_done, n + 1)
                            if n >= 8:
                                dve.wait_ge(R_ready, n - 7)
                            if n not in ranked:
                                limit = -1.0 if fast else -FMAX
                            elif fast:
                                dve.wait_ge(picked_done, n + 1 - FIRST_TOP)
                                limit = kth[:, n % 8:n % 8 + 1]
                            else:
                                dve.wait_ge(tk, dep[n])
                                limit = top[n % 2][:, TOPK - 1:TOPK]
                            step(nc.vector.scalar_tensor_tensor(
                                out=E[n % 4][:, 0:w], in0=S[n % SBUFS][:, 0:w], scalar=limit, in1=E[n % 4][:, 0:w],
                                op0=ALU.is_ge, op1=ALU.mult, accum_out=rsum[:, n % 8:n % 8 + 1]), n, dep)
                        for n in both:
                            dve.wait_ge(tk, dep[n])
                            nc.vector.reciprocal(rinv[:, n % 8:n % 8 + 1], rsum[:, n % 8:n % 8 + 1]).then_inc(E_ready, 1)

                    chain.n = 0
                    for n0 in range(0, GPB, 2):
                        t, g = divmod(n0, GPT)
                        top_pair(n0)
                        if g == 0:
                            dve_ln_stats(dve, t + 1)
                        if g == 2 and t:
                            gate_tile(t - 1)
                        if g == 4:
                            dve_ln_apply(dve, t + 1)
                        if g == 6:
                            if t:
                                residual(t - 1)
                            dve_ssq(dve, t + 1, 0)
                        if g == 8:
                            dve_ssq(dve, t + 1, 1)
                    if fast:
                        middle = (WINDOW - 1) / 2
                        off = rank[:, FIRST_TOP:GPB]
                        chain(dve, nc.vector.tensor_scalar(off, off, -ROUND, -middle, ALU.add, ALU.add))
                        chain(dve, nc.vector.tensor_tensor(off, off, off, ALU.mult))
                        chain(dve, nc.vector.reduce_max(worst[:, 0:1], off, axis=AX.X))
                        chain(dve, nc.vector.reduce_max(worst[:, 1:2], sumsq[:, FIRST_TOP:GPB + 1], axis=AX.X))
                        chain(dve, nc.vector.tensor_scalar(flag[:, :], worst[:, 1:2], SUMSQ_LIMIT, None, ALU.is_gt))
                        nc.vector.scalar_tensor_tensor(out=flag[:, :], in0=worst[:, 0:1], scalar=(middle + 0.1) ** 2,
                                                       in1=flag[:, :], op0=ALU.is_gt, op1=ALU.max) \
                            .then_inc(flagged, 1)
                    gate_tile(TPB - 1)
                    residual(TPB - 1)
                    if fast:
                        dve.wait_ge(flag_sum, 1)
                        nc.vector.tensor_scalar(again[:, :], bankA[:, 0:1], 0.5, None, ALU.is_gt).then_inc(tk, 1)

        def clear():
            with nc.Block() as block:
                @block.gpsimd
                def _(pool):
                    numbers = sorted(s.num for s in counters.values())
                    assert numbers == list(range(numbers[0], numbers[-1] + 1))
                    pool.sem_clear(range(numbers[0], numbers[-1] + 1))

        body("first", None)
        clear()
        with nc.Fori(0, B) as b:
            body("fast", b)
            clear()
            need = nc.values_load(again[0:1, 0:1], min_val=0, max_val=1)
            with nc.If(need > 0):
                body("first", b)
                clear()
                body("slow", b)
                clear()


def bcast(ap, pattern, offset=0):
    return bass.AP(tensor=ap.tensor, offset=ap.offset + offset, ap=pattern)


def build(nc, a, out):
    x1_dram = nc.dram_tensor("x1", ((TILES + 1) * P, D), F32, kind="Internal").ap()
    x2_dram = nc.dram_tensor("x2", (TILES * P, D), F32, kind="Internal").ap()
    rows = "b n d -> (b n) d"
    with ExitStack() as ctx:
        W = Weights()
        place_weights(nc, ctx, W)
        names = ("Wq", "Wk", "Wv", "Wg")
        token_weights = [ctx.enter_context(nc.sbuf_tensor(n, [P, 2, HD], F32)) for n in names]
        with nc.sbuf_tensor("X_first", [P, TILES, D], F32) as X:
            setup_phase(nc, W, X, {**a, "x": a["x"].rearrange(rows)}, x1_dram)
            ffn_phase(nc, "ffn1", X, W, None, x1_dram,
                      [(w[:, :, :], a[n].rearrange("(k p) n -> p k n", p=P)) for w, n in zip(token_weights, names)])
        attention_phase(nc, W, token_weights, a, x1_dram, x2_dram)
        with nc.sbuf_tensor("X_last", [P, TILES, D], F32) as X:
            ffn_phase(nc, "ffn2", X, W, x2_dram, out.rearrange(rows))


NAMES = {'x': 'L0_attn_x', 'Wq': 'L0_attn_Wq', 'Wk': 'L0_attn_Wk', 'Wv': 'L0_attn_Wv', 'Wg': 'L0_attn_Wg',
         'bg': 'L0_attn_bg', 'Wo': 'L0_attn_Wo', 'W_pre_th': 'L0_attn_W_pre_th',
         'W_post_th': 'L0_attn_W_post_th', 'mem_k': 'L0_attn_mem_k', 'mem_v': 'L0_attn_mem_v',
         'head_scale': 'L0_attn_head_scale_params', 'adaptive_range': 'L0_ffn_adaptive_range',
         **{f'cn_{k}{i}': f'L0_ffn_cn_{k}{i}' for k in 'wb' for i in (1, 2, 3, 4)},
         **{f'gc_{k}{i}': f'L0_ffn_gc_{k}{i}' for k in 'wb' for i in (1, 2, 3)}}


class Inputs:
    pass


def kernel(**inputs):
    import numpy as _np
    import concourse.bacc as _bacc
    from concourse import mybir as _mybir
    from concourse.bass_utils import run_bass_kernel_spmd as _run

    nc = _bacc.Bacc("TRN2", target_bir_lowering=False, num_devices=1)
    arrays, aps = {}, {}
    for short, name in NAMES.items():
        arr = _np.ascontiguousarray(inputs[name])
        arrays[f"in_{name}_dram"] = arr
        aps[short] = nc.dram_tensor(f"in_{name}_dram", arr.shape, _mybir.dt.from_np(arr.dtype),
                                    kind="ExternalInput").ap()
    out = nc.dram_tensor("out_0_dram", (B, N, D), _mybir.dt.float32, kind="ExternalOutput").ap()
    build(nc, aps, out)
    r = _run(nc, [arrays], core_ids=[0])
    return r.results[0]["out_0_dram"]
```
